# Optimizing a Trainium2 kernel written in Bass

```python
import numpy as np
import jax
import jax.numpy as jnp

def _softmax(x, axis=-1):
    return jax.nn.softmax(x, axis=axis)

def _gelu(x):
    return jax.nn.gelu(x, approximate=True)

def _silu(x):
    return jax.nn.silu(x)

def _sigmoid(x):
    return jax.nn.sigmoid(x)

def _layernorm(x, axis=-1, eps=1e-05):
    m = jnp.mean(x, axis=axis, keepdims=True)
    v = jnp.var(x, axis=axis, keepdims=True)
    return (x - m) / jnp.sqrt(v + eps)

def _scatter_add(tgt, idx, src, axis=0):
    return tgt.at[idx].add(src)

def _segment_sum(src, seg, n):
    return jax.ops.segment_sum(src, seg, n)
kernel_name = 'mk_adaln_d1_jaxref_r4_2244f2'

def setup_inputs(seed: int=0):
    np.random.seed(seed)
    _w = jnp.asarray

    def _L0_attn_setup():
        import jax, jax.numpy as jnp
        import numpy as np
        N_HEADS = 32
        WINDOW = 128

        def _sliding_window_attention(x, Wq, Wk, Wv, Wo, n_heads=N_HEADS, window=WINDOW):
            B, T, D = x.shape
            H, dk = (n_heads, D // n_heads)
            bs = window
            assert T % bs == 0
            nb = T // bs

            def heads(y):
                return y.reshape(B, T, H, dk).transpose(0, 2, 1, 3)
            q = heads(x @ Wq.T)
            k = heads(x @ Wk.T)
            v = heads(x @ Wv.T)
            qb = q.reshape(B, H, nb, bs, dk)
            zpad = jnp.zeros((B, H, bs, dk), dtype=x.dtype)
            kp = jnp.concatenate([zpad, k], axis=2).reshape(B, H, nb + 1, bs, dk)
            vp = jnp.concatenate([zpad, v], axis=2).reshape(B, H, nb + 1, bs, dk)
            kw = jnp.concatenate([kp[:, :, :-1], kp[:, :, 1:]], axis=3)
            vw = jnp.concatenate([vp[:, :, :-1], vp[:, :, 1:]], axis=3)
            scale = 1.0 / np.sqrt(dk).astype(np.float32)
            scores = jnp.einsum('bhnrd,bhncd->bhnrc', qb, kw) * scale
            i = jnp.arange(nb)[:, None, None]
            r = jnp.arange(bs)[None, :, None]
            c = jnp.arange(2 * bs)[None, None, :]
            dist = bs + r - c
            key_global = i * bs - bs + c
            valid = (dist >= 0) & (dist <= window) & (key_global >= 0)
            scores = jnp.where(valid[None, None], scores, jnp.finfo(scores.dtype).min)
            probs = jax.nn.softmax(scores, axis=-1)
            out = jnp.einsum('bhnrc,bhncd->bhnrd', probs, vw)
            out = out.reshape(B, H, T, dk).transpose(0, 2, 1, 3).reshape(B, T, D)
            return out @ Wo.T
        key = jax.random.key(seed)
        ks = jax.random.split(key, 5)
        B, T, D = (2, 1024, 512)
        w_std = 0.02
        return {'x': jax.random.normal(ks[0], (B, T, D), dtype=jnp.float32), 'Wq': jax.random.normal(ks[1], (D, D), dtype=jnp.float32) * w_std, 'Wk': jax.random.normal(ks[2], (D, D), dtype=jnp.float32) * w_std, 'Wv': jax.random.normal(ks[3], (D, D), dtype=jnp.float32) * w_std, 'Wo': jax.random.normal(ks[4], (D, D), dtype=jnp.float32) * w_std}
    _L0_attn_in = _L0_attn_setup()

    def _L0_ffn_setup():
        import jax, jax.numpy as jnp
        import numpy as np
        FP8_MAX = 448.0
        SCALE_MARGIN = 0.8

        def _fp8_quant_dequant(t, scale):
            q = (t / scale).astype(jnp.float8_e4m3fn)
            return q.astype(jnp.float32) * scale
        key = jax.random.key(seed)
        k1, k2 = jax.random.split(key)
        B, S, D_IN, D_OUT = (4, 512, 512, 512)
        x = jax.random.normal(k1, (B, S, D_IN), dtype=jnp.float32)
        weight = jax.random.normal(k2, (D_OUT, D_IN), dtype=jnp.float32)
        bias = jnp.zeros((D_OUT,), dtype=jnp.float32)
        return {'x': x, 'weight': weight, 'bias': bias}
    _L0_ffn_in = _L0_ffn_setup()
    _L0_c = _w((lambda *s: np.random.randn(*s).astype(np.float32) * 0.05)(1, 512))
    _L0_wmod = _w((lambda *s: np.random.randn(*s).astype(np.float32) * 0.05)(512, 6 * 512) * 512 ** (-0.5))
    _d = {'L0_attn_x': _L0_attn_in['x'], 'L0_attn_Wq': _L0_attn_in['Wq'], 'L0_attn_Wk': _L0_attn_in['Wk'], 'L0_attn_Wv': _L0_attn_in['Wv'], 'L0_attn_Wo': _L0_attn_in['Wo'], 'L0_ffn_weight': _L0_ffn_in['weight'], 'L0_ffn_bias': _L0_ffn_in['bias'], 'L0_c': _L0_c, 'L0_wmod': _L0_wmod}
    _x0 = _d['L0_attn_x']
    _d['L0_attn_x'] = jax.random.normal(jax.random.fold_in(jax.random.key(seed), 1), (1, 4096, 512), dtype=_x0.dtype)
    del _x0
    return _d

def reference(L0_attn_x, L0_attn_Wq, L0_attn_Wk, L0_attn_Wv, L0_attn_Wo, L0_ffn_weight, L0_ffn_bias, L0_c, L0_wmod):

    def _L0_attn_ref(x, Wq, Wk, Wv, Wo):
        import jax, jax.numpy as jnp
        import numpy as np
        N_HEADS = 32
        WINDOW = 128

        def _sliding_window_attention(x, Wq, Wk, Wv, Wo, n_heads=N_HEADS, window=WINDOW):
            B, T, D = x.shape
            H, dk = (n_heads, D // n_heads)
            bs = window
            assert T % bs == 0
            nb = T // bs

            def heads(y):
                return y.reshape(B, T, H, dk).transpose(0, 2, 1, 3)
            q = heads(x @ Wq.T)
            k = heads(x @ Wk.T)
            v = heads(x @ Wv.T)
            qb = q.reshape(B, H, nb, bs, dk)
            zpad = jnp.zeros((B, H, bs, dk), dtype=x.dtype)
            kp = jnp.concatenate([zpad, k], axis=2).reshape(B, H, nb + 1, bs, dk)
            vp = jnp.concatenate([zpad, v], axis=2).reshape(B, H, nb + 1, bs, dk)
            kw = jnp.concatenate([kp[:, :, :-1], kp[:, :, 1:]], axis=3)
            vw = jnp.concatenate([vp[:, :, :-1], vp[:, :, 1:]], axis=3)
            scale = 1.0 / np.sqrt(dk).astype(np.float32)
            scores = jnp.einsum('bhnrd,bhncd->bhnrc', qb, kw) * scale
            i = jnp.arange(nb)[:, None, None]
            r = jnp.arange(bs)[None, :, None]
            c = jnp.arange(2 * bs)[None, None, :]
            dist = bs + r - c
            key_global = i * bs - bs + c
            valid = (dist >= 0) & (dist <= window) & (key_global >= 0)
            scores = jnp.where(valid[None, None], scores, jnp.finfo(scores.dtype).min)
            probs = jax.nn.softmax(scores, axis=-1)
            out = jnp.einsum('bhnrc,bhncd->bhnrd', probs, vw)
            out = out.reshape(B, H, T, dk).transpose(0, 2, 1, 3).reshape(B, T, D)
            return out @ Wo.T
        return _sliding_window_attention(x, Wq, Wk, Wv, Wo)

    def _L0_ffn_ref(x, weight, bias):
        import jax, jax.numpy as jnp
        import numpy as np
        FP8_MAX = 448.0
        SCALE_MARGIN = 0.8

        def _fp8_quant_dequant(t, scale):
            q = (t / scale).astype(jnp.float8_e4m3fn)
            return q.astype(jnp.float32) * scale
        amax_x = jnp.max(jnp.abs(x))
        amax_w = jnp.max(jnp.abs(weight))
        x_scale = amax_x / (FP8_MAX * SCALE_MARGIN)
        w_scale = jnp.maximum(amax_x, amax_w) / (FP8_MAX * SCALE_MARGIN)
        x_scale = jax.lax.stop_gradient(x_scale)
        w_scale = jax.lax.stop_gradient(w_scale)
        x_dq = _fp8_quant_dequant(x, x_scale)
        w_dq = _fp8_quant_dequant(weight, w_scale)
        out = jnp.einsum('bsd,od->bso', x_dq, w_dq)
        return out + bias
    x = L0_attn_x
    mod = (_silu(L0_c) @ L0_wmod).reshape(L0_c.shape[0], 6, 1, -1)
    sa, ca, ga, sb, cb, gb = (mod[:, 0], mod[:, 1], mod[:, 2], mod[:, 3], mod[:, 4], mod[:, 5])
    ga = (2 * (ga >= 0) - 1) * jnp.maximum(jnp.abs(ga), 0.25)
    gb = (2 * (gb >= 0) - 1) * jnp.maximum(jnp.abs(gb), 0.25)
    h = _layernorm(x, axis=-1) * (1 + ca) + sa
    x = x + ga * _L0_attn_ref(h, L0_attn_Wq, L0_attn_Wk, L0_attn_Wv, L0_attn_Wo)
    h = _layernorm(x, axis=-1) * (1 + cb) + sb
    x = x + gb * _L0_ffn_ref(h, L0_ffn_weight, L0_ffn_bias)
    return x

_drawn_inputs = setup_inputs


def setup_inputs(seed=0):
    import zlib

    import numpy as np

    out = dict(_drawn_inputs(seed))
    spreads = {'L0_ffn_bias': (0.0, 0.8)}
    factors = {'L0_attn_Wq': 8.0, 'L0_attn_Wk': 7.976, 'L0_attn_Wv': 4.061, 'L0_attn_Wo': 4.188}
    for name, (base, spread) in spreads.items():
        noise = np.random.default_rng([zlib.crc32(name.encode()), seed]).standard_normal(out[name].shape)
        drawn = base * np.exp(spread * noise) if base else spread * noise
        out[name] = jnp.asarray(drawn.astype(out[name].dtype))
    for name, factor in factors.items():
        out[name] = (out[name] * factor).astype(out[name].dtype)
    return out
```

```python
import concourse.bass as bass
from concourse import mybir
from contextlib import ExitStack


class Count:

    def __init__(self, k, a, b):
        self.k, self.a, self.b = k, (a if k is not None else 0), b

    def __mul__(self, m):
        return Count(self.k, self.a * m, self.b * m)

    def __add__(self, n):
        return Count(self.k, self.a, self.b + n)

    def __sub__(self, n):
        return self + (-n)

    def half(self):
        return Count(self.k, self.a // 2, self.b // 2)

    @property
    def parity(self):
        return self.b % 2

    def within(self, lo, hi):
        return True if self.k is not None else lo <= self.b < hi

    def value(self):
        return self.b if self.k is None or self.a == 0 else self.k * self.a + self.b


def need(eng, sem, count, apart=False):
    if isinstance(count, Count):
        if count.k is None and count.b <= 0:
            return
        assert count.b > 0, "a looped turn waits for something"
        eng.wait_ge(sem, count.value())
        if apart and count.k is not None:
            eng.nop(nofuse=True)
    elif count > 0:
        eng.wait_ge(sem, count)


def adaln_block(nc: bass.Bass, x, Wq, Wk, Wv, Wo, Wf, bias, c, wmod, out):
    fp32 = mybir.dt.float32
    fp32r = mybir.dt.float32r
    bf16 = mybir.dt.bfloat16
    u32 = mybir.dt.uint32
    ALU = mybir.AluOpType
    ACT = mybir.ActivationFunctionType
    AX = mybir.AxisListType.X

    T, D = x.shape[1], x.shape[2]
    H, DK = 32, D // 32
    W = 128
    KT = D // 128
    NB = T // W
    ST = 2 * W
    NS = T // ST
    SK = W + 32
    SG = 3
    NSG = (H + SG - 1) // SG
    NPAIR = H // 2
    RING = 4
    HR = DK + 1
    KROWS = 6 * DK
    EPS = 1e-5
    SCALE = 1.0 / DK ** 0.5
    QMAX = 448.0 * 0.8
    LOW = -3.0e38

    xs = x.rearrange("a (s b p) d -> (a s) p b d", b=2, p=128)
    xb = x.rearrange("a (n p) d -> (a n) p d", p=128)
    ob = out.rearrange("a (n p) d -> (a n) p d", p=128)

    ctx = ExitStack()
    with ctx:
        def sb(name, shape, dt):
            return ctx.enter_context(nc.sbuf_tensor(name, shape, dt))

        def sem(name):
            return ctx.enter_context(nc.semaphore(name))

        q_parts_dram = nc.dram_tensor("q_parts", [3, D, T], bf16, kind="Internal").ap()
        k_parts_dram = nc.dram_tensor("k_parts", [3, D, T], bf16, kind="Internal").ap()
        x1_dram = nc.dram_tensor("x1_scratch", [NB, 128, D], fp32, kind="Internal").ap()
        h2_dram = nc.dram_tensor("h2_scratch", [NB, 128, D], fp32, kind="Internal").ap()
        parts_dram = {"q": q_parts_dram, "k": k_parts_dram}

        w_hi = {n: sb(f"w{n}_hi", [128, KT, D], fp32r) for n in "qkvo"}
        w_lo = {n: sb(f"w{n}_lo", [128, KT, D], fp32r) for n in "qkvo"}
        Q_SLOTS, K_SLOTS = (0, 0, 0, 1, 1, 2), (0, 1, 2, 0, 1, 0)
        stacks = sb("stacks", [128, H * (2 * ST + W + 2 * ST)], bf16)
        q_stack = stacks[:, 0:2 * H * ST].rearrange("p (r h t) -> p r h t", r=2, h=H)
        k_stack = stacks[:, 2 * H * ST:].rearrange("p (h t) -> p h t", h=H)

        x_in = sb("x_in", [128, 2, 2, D], fp32)
        hT_hi = sb("hT_hi", [128, KT, ST], fp32r)
        hT_lo = sb("hT_lo", [128, KT, ST], fp32r)
        parts = sb("parts", [128, 2, 3, 2, ST], bf16)
        rest = sb("rest", [128, 2, ST], fp32)
        v_tok = sb("v_tok", [128, 5, H, HR], fp32)
        probs = sb("probs", [128, RING, 4, W], fp32)
        cb1_row = sb("cb1_row", [128, D], fp32)
        sb_row = sb("sb_row", [128, D], fp32)
        gb_row = sb("gb_row", [128, D], fp32)
        vb_row = sb("vb_row", [128, D], fp32)
        work = sb("work", [128, 2 * D + 2 * D], fp32)
        x1 = work[:, 0:2 * D].rearrange("p (r d) -> p r d", r=2)
        heads_sb = work[:, 2 * D:4 * D].rearrange("p (f g t) -> p f g t", f=2, g=4)
        h2 = sb("h2", [128, 2, D], fp32)
        attn = sb("attn", [128, D], fp32)
        attnT_hi = sb("attnT_hi", [128, KT, W], fp32r)
        attnT_lo = sb("attnT_lo", [128, KT, W], fp32r)
        ident_f = sb("ident_f", [128, 128], fp32)
        ident_b = sb("ident_b", [128, 128], bf16)
        mask = sb("mask", [128, SK], bf16)
        maskT = sb("maskT", [128, 2, W], bf16)
        first_masks = h2[:, 0, :].bitcast(bf16)
        mask_first = first_masks[:, 0:SK]
        maskT_first = first_masks[:, 2 * W:4 * W].rearrange("p (f t) -> p f t", f=2)
        row_max = sb("row_max", [128, H], fp32)
        r_den = sb("r_den", [128, H], fp32)
        mT = sb("mT", [H, 2, W], bf16)
        stats = sb("stats", [128, 3, 6], fp32)
        mv = sb("mv", [128, 3, 2], fp32)
        rstd = sb("rstd", [128, 3], fp32)
        m_half = sb("m_half", [128, 3], fp32)
        h2_max = sb("h2_max", [128, NB], fp32)
        cols = sb("cols", [128, 3, KT], fp32)
        c_col = sb("c_col", [128, 4, KT], fp32)
        g_tmp = sb("g_tmp", [128, 2, KT], fp32)
        w_scale = sb("w_scale", [128, 2, KT], fp32)
        qk_bias = sb("qk_bias", [128, 2, KT], fp32)
        q8 = sb("q8", [128, 8], fp32)

        ps = ctx.enter_context(nc.psum_tensor("ps", [128, 8, 512], fp32))
        st_ps = [ps[:, 0 + b, :].rearrange("p (f t) -> p f t", f=4) for b in range(2)]
        s_ps = [ps[:, 2 + b, 0:SG * SK].rearrange("p (h t) -> p h t", h=SG) for b in range(2)]
        heads_ps = [ps[:, 4 + b, :].rearrange("p (g t) -> p g t", g=4) for b in range(2)]
        misc_ps = [ps[:, 6 + b, :] for b in range(2)]

        c_loaded = sem("c_loaded")
        wmod_loaded = sem("wmod_loaded")
        w_loaded = {n: sem(f"w{n}_loaded") for n in "qkvo"}
        consts_step = sem("consts_step")
        consts_ready = sem("consts_ready")
        first_masks_ready = sem("first_masks_ready")
        silu_exp = sem("silu_exp")
        setup_chain = sem("setup_chain")
        silu_ready = sem("silu_ready")
        mod_cols_full = sem("mod_cols_full")
        mod_rows_full = sem("mod_rows_full")
        mod_ready = sem("mod_ready")
        rows_ready = sem("rows_ready")
        wT_full = sem("wT_full")
        wT_copied = sem("wT_copied")
        wT_split = sem("wT_split")
        wb_full = sem("wb_full")
        setup_done = sem("setup_done")
        x_loaded = [sem("x_loaded_even"), sem("x_loaded_odd")]
        x1_loaded = [sem("xres_loaded_0"), sem("xres_loaded_1")]
        ln1_stats = sem("ln1_stats")
        ln1_mv = sem("ln1_mv")
        ln1_eps = sem("ln1_eps")
        ln1_rstd = sem("ln1_rstd")
        xhat_ready = sem("xhat_ready")
        xT_full = sem("xT_full")
        hT_hi_ready = sem("hT_hi_ready")
        hT_ready = sem("hT_ready")
        qk_full = sem("qk_full")
        qk_hi_ready = sem("qk_hi_ready")
        qk_rest_ready = sem("qk_rest_ready")
        qk_mid_ready = sem("qk_mid_ready")
        qk_lo_ready = sem("qk_lo_ready")
        parts_stored = [sem("parts_stored_0"), sem("parts_stored_1")]
        q_loaded = sem("q_loaded")
        k_loaded = [sem("k_loaded_0"), sem("k_loaded_1")]
        k_carry_loaded = sem("k_carry_loaded")
        v_full = sem("v_full")
        v_ready = sem("v_ready")
        s_full = sem("s_full")
        max_done = sem("max_done")
        mT_full = sem("mT_full")
        mT_hi_ready = sem("mT_hi_ready")
        mT_ready = sem("mT_ready")
        m_loaded = sem("m_loaded")
        st_full = sem("st_full")
        exp_done = sem("exp_done")
        pv_done = sem("pv_done")
        heads_copied = sem("heads_copied")
        headsT_full = sem("headsT_full")
        den_ready = sem("den_ready")
        attn_ready = sem("attn_ready")
        attnT_full = sem("attnT_full")
        attnT_hi_ready = sem("attnT_hi_ready")
        attnT_ready = sem("attnT_ready")
        y_full = sem("y_full")
        x1_ready = sem("x1_ready")
        ln2_stats = sem("ln2_stats")
        ln2_mv = sem("ln2_mv")
        ln2_eps = sem("ln2_eps")
        ln2_rstd = sem("ln2_rstd")
        x1hat_ready = sem("x1hat_ready")
        h2_scaled = sem("h2_scaled")
        h2_ready = sem("h2_ready")
        h2_max_done = sem("h2_max_done")
        x1_stored = [sem("x1_stored_0"), sem("x1_stored_1")]
        h2_stored = [sem("h2_stored_0"), sem("h2_stored_1")]

        USES = [("headsT", 0, 1), ("xT", 0, 0), ("xT", 0, 1), ("attnT", 0, 0), ("qk", 0, 0), ("qk", 0, 1),
                ("y", 0, 0), ("qk", 0, 2), ("qk", 0, 3), ("headsT", 0, 0), ("mT", 0, 0),
                ("headsT", 1, 1), ("v", 1, 0), ("attnT", 1, 0), ("v", 1, 1), ("y", 1, 0), ("headsT", 1, 0),
                ("mT", 1, 0)]
        FREED = {"xT": hT_ready, "qk": qk_rest_ready, "v": v_ready, "headsT": attn_ready,
                 "attnT": attnT_ready, "y": x1_ready, "mT": mT_ready}

        def nth(s, use):
            kind, b, n = use
            if kind in ("xT", "v"):
                return s * 2 + (2 + n), 2 * NS
            if kind == "qk":
                return s * 4 + (4 + n), 4 * NS
            if kind == "headsT":
                return s * 4 + (2 * b + n if n == 0 else 2 * b - 1), 2 * NB
            if kind in ("attnT", "y"):
                return s * 2 + (b - 1), NB
            return s * 2 + (b + 1), NB

        def misc_bank(pe, s, use):
            at = USES.index(use)
            pos, back = at, s
            while True:
                pos -= 2
                if pos < 0:
                    pos, back = pos + len(USES), back - 1
                if back.k is None and back.b < -1:
                    break
                n, total = nth(back, USES[pos])
                if n.within(0, total):
                    need(pe, FREED[USES[pos][0]], n + 1)
                    break
            return misc_ps[at % 2]

        def turns(eng, body):
            body(Count(None, 0, -1))
            body(Count(None, 0, 0))
            with eng.Fori(0, (NS - 4) // 2) as k:
                body(Count(k, 2, 1))
                body(Count(k, 2, 2))
            for s in range(NS - 3, NS + 1):
                body(Count(None, 0, s))

        def k_at(s, b):
            return ST * s.parity + W * b

        first_phase = ExitStack()
        block = first_phase.enter_context(nc.Block())
        wmod_sb = stacks[:, 0:2 * KT * 6 * D].bitcast(fp32).rearrange("p (k n) -> p k n", k=KT)
        wst = stacks[:, 2 * KT * 6 * D:2 * KT * 6 * D + 6 * KT * D].bitcast(fp32).rearrange(
            "p (w k d) -> p w k d", w=3, k=KT)
        w_nat = {"q": wst[:, 0], "k": wst[:, 1], "v": wst[:, 2],
                 "o": probs[:].rearrange("p r f t -> p (r f t)").rearrange("p (k d) -> p k d", k=KT)}
        wT = work[:].rearrange("p (k d) -> p k d", k=KT)
        silu_bc = attn[:].rearrange("p (k m) -> p k m", k=KT)
        sa_bc = h2[:, 0, :].rearrange("p (k m) -> p k m", k=KT)
        MATS = ("v", "q", "k", "o")

        @block.sync
        def _(sp):
            with nc.allow_non_contiguous_dma(reason="512 values, once"):
                sp.dma_start(c_col[:, 0, :], c.rearrange("a (k p) -> p (a k)", p=128)).then_inc(c_loaded, 16)
            wmod_v = wmod.rearrange("(k p) n -> p k n", p=128)
            for n in range(6):
                sp.dma_start(wmod_sb[:, :, n * D:(n + 1) * D], wmod_v[:, :, n * D:(n + 1) * D]).then_inc(wmod_loaded, 16)
            for n, w in (("v", Wv), ("q", Wq), ("k", Wk), ("o", Wo)):
                sp.dma_start(w_nat[n], w.rearrange("(k p) d -> p k d", p=128)).then_inc(w_loaded[n], 16)
            for s in range(2):
                sp.dma_start(x_in[:, s], xs[s]).then_inc(x_loaded[s], 16)
            sp.wait_ge(setup_done, 1)

            def store_parts(s, g):
                t = s + 1
                need(sp, qk_lo_ready, t * 4 + (g + 1), apart=True)
                dram = parts_dram["q" if g < 2 else "k"]
                for part in range(3):
                    rows = dram[part, (g % 2) * 2 * 128:((g % 2) * 2 + 2) * 128, :].rearrange("(m p) t -> p m t", p=128)
                    sp.dma_start(rows[:, :, bass.ds((t * ST).value(), ST)],
                                 parts[:, g % 2, part]).then_inc(parts_stored[g % 2], 16)

            def load_stack(dst, name, slots, start, n, done):
                for row, part in enumerate(slots):
                    src = parts_dram[name][part].rearrange("(h d) t -> d h t", d=DK)
                    sp.dma_start(dst[row * DK:(row + 1) * DK], src[:, :, bass.ds(start, n)]).then_inc(done, 16)

            def body(s):
                t = s + 1
                for b in range(2):
                    i = s * 2 + b
                    if i.within(0, NB):
                        need(sp, h2_stored[b], s * 16, apart=True)
                        need(sp, x1_stored[b], s * 16, apart=True)
                        sp.dma_start(x1[:, b, :], xb[bass.ds(i.value(), 1)].rearrange("a p d -> p (a d)")
                                     ).then_inc(x1_loaded[b], 16)
                    if b == 0 and t.within(0, NS):
                        store_parts(s, 0)
                        store_parts(s, 1)
                        need(sp, parts_stored[0], t * 96 + 48, apart=True)
                        need(sp, parts_stored[1], t * 96 + 48, apart=True)
                        need(sp, st_full, s * (2 * NPAIR), apart=True)
                        load_stack(q_stack[:, t.parity], "q", Q_SLOTS, (t * ST).value(), ST, q_loaded)
                        store_parts(s, 2)
                        store_parts(s, 3)
                        need(sp, parts_stored[0], t * 96 + 96, apart=True)
                        need(sp, parts_stored[1], t * 96 + 96, apart=True)
                        load_stack(k_stack[:, :, k_at(t, 0) + W:k_at(t, 0) + 2 * W], "k", K_SLOTS,
                                   (t * ST).value(), W, k_loaded[0])
                    if b == 1 and (s + 3).within(2, NS):
                        need(sp, xT_full, t * 2 + 2, apart=True)
                        load_x(s + 3)
                    j = i + 1
                    if (i - 1).within(0, NB):
                        store_block(i - 1, (b + 1) % 2, s if b else s - 1)
                    if j.within(0, NB):
                        need(sp, mT_ready, j + 1, apart=True)
                        jb = (b + 1) % 2
                        jp = s.parity if b == 0 else t.parity
                        for part in range(2):
                            sp.dma_start(q_stack[KROWS + part:KROWS + part + 1, jp, :, jb * W:(jb + 1) * W],
                                         mT[:, part, :]).then_inc(m_loaded, 16)
                    if b == 0 and t.within(0, NS):
                        need(sp, st_full, (s * 2 + 1) * NPAIR, apart=True)
                        load_stack(k_stack[:, :, k_at(t, 1) + W:k_at(t, 1) + 2 * W], "k", K_SLOTS,
                                   (t * ST + W).value(), W, k_loaded[1])
                        if t.parity:
                            load_stack(k_stack[:, :, 0:W], "k", K_SLOTS, (t * ST + W).value(), W, k_carry_loaded)

            def load_x(t):
                sp.dma_start(x_in[:, t.parity],
                             xs[bass.ds(t.value(), 1)].rearrange("a p b d -> p (a b) d")).then_inc(x_loaded[t.parity], 16)

            def store_block(i, b, s):
                need(sp, ln2_mv, i + 1, apart=True)
                need(sp, x1hat_ready, i + 1, apart=True)
                sp.dma_start(x1_dram[bass.ds(i.value(), 1)].rearrange("a p d -> p (a d)"), x1[:, b, :]).then_inc(x1_stored[b], 16)
                need(sp, h2_ready, i + 1, apart=True)
                sp.dma_start(h2_dram[bass.ds(i.value(), 1)].rearrange("a p d -> p (a d)"), h2[:, b, :]).then_inc(h2_stored[b], 16)

            turns(sp, body)
            for b in range(2):
                sp.wait_ge(x1_stored[b], 16 * (NB // 2))
                sp.wait_ge(h2_stored[b], 16 * (NB // 2))

        @block.gpsimd
        def _(pool):
            done = [0]

            def link(ins):
                done[0] += 1
                ins.then_inc(consts_step, 1)
                pool.wait_ge(consts_step, done[0])

            link(nc.gpsimd.memset(ident_f[:], 1.0))
            link(nc.gpsimd.affine_select(out=ident_f[:], in_=ident_f[:], compare_op=ALU.is_equal, fill=0.0, base=0,
                                         pattern=[[-1, 128]], channel_multiplier=1))
            link(nc.gpsimd.tensor_scalar(ident_b[:], ident_f[:], 1.0, None, ALU.mult))
            link(nc.gpsimd.memset(m_half[:], -0.5))
            link(nc.gpsimd.memset(mask[:], 0.0))
            for g in range(4):
                rows = mask[32 * g:32 * g + 32, :]
                link(nc.gpsimd.affine_select(out=rows, in_=rows, compare_op=ALU.is_ge, fill=LOW, base=0,
                                             pattern=[[1, SK]], channel_multiplier=-1))
                link(nc.gpsimd.affine_select(out=rows, in_=rows, compare_op=ALU.is_ge, fill=LOW, base=W,
                                             pattern=[[-1, SK]], channel_multiplier=1))
            link(nc.gpsimd.memset(maskT[:], 0.0))
            link(nc.gpsimd.affine_select(out=maskT[:, 0], in_=maskT[:, 0], compare_op=ALU.is_ge, fill=LOW, base=0,
                                         pattern=[[-1, W]], channel_multiplier=1))
            link(nc.gpsimd.affine_select(out=maskT[:, 1], in_=maskT[:, 1], compare_op=ALU.is_ge, fill=LOW, base=0,
                                         pattern=[[1, W]], channel_multiplier=-1))
            nc.gpsimd.memset(v_tok[:], 1.0).then_inc(consts_ready, 1)

            def inv_std(at, mv_ready, eps_added, ready, n, first, last):
                need(pool, mv_ready, n, apart=True)
                nc.gpsimd.tensor_scalar(rstd[:, first:last], mv[:, first:last, 1], EPS, None, ALU.add).then_inc(eps_added, 1)
                need(pool, eps_added, at, apart=True)
                nc.gpsimd.tensor_tensor(rstd[:, first:last], rstd[:, first:last], m_half[:, first:last],
                                        ALU.pow).then_inc(ready, 1)

            def ln1(t):
                inv_std(t + 1, ln1_mv, ln1_eps, ln1_rstd, t * 2 + 2, 0, 2)

            def body(s):
                t = s + 1
                for b in range(2):
                    i = s * 2 + b
                    if b == 0 and t.within(0, NS):
                        for g in range(4):
                            n = t * 4 + (g + 1)
                            need(pool, qk_rest_ready, n, apart=True)
                            nc.gpsimd.tensor_scalar(parts[:, g % 2, 1], rest[:], 1.0, None, ALU.mult).then_inc(qk_mid_ready, 1)
                            need(pool, qk_mid_ready, n, apart=True)
                            nc.gpsimd.tensor_tensor(parts[:, g % 2, 2], rest[:], parts[:, g % 2, 1],
                                                    ALU.subtract).then_inc(qk_lo_ready, 1)
                            if g == 1 and (i - 1).within(0, NB):
                                inv_std(i, ln2_mv, ln2_eps, ln2_rstd, i, 2, 3)
                    elif (i - 1).within(0, NB):
                        inv_std(i, ln2_mv, ln2_eps, ln2_rstd, i, 2, 3)
                    if b == 1 and (s + 2).within(0, NS):
                        ln1(s + 2)
                    if (i - 1).within(0, NB):
                        hb = (b + 1) % 2
                        need(pool, x1hat_ready, i, apart=True)
                        nc.gpsimd.tensor_tensor(h2[:, hb], h2[:, hb], cb1_row[:], ALU.mult).then_inc(h2_scaled, 1)
                        need(pool, h2_scaled, i, apart=True)
                        nc.gpsimd.tensor_tensor(h2[:, hb], h2[:, hb], sb_row[:], ALU.add).then_inc(h2_ready, 1)

            pool.wait_ge(setup_done, 1)
            link(nc.gpsimd.tensor_scalar(mask_first, mask[:], 1.0, None, ALU.mult))
            for g in range(4):
                rows = mask_first[32 * g:32 * g + 32, :]
                link(nc.gpsimd.affine_select(out=rows, in_=rows, compare_op=ALU.is_ge, fill=LOW, base=32 * g - W,
                                             pattern=[[1, SK]], channel_multiplier=0))
            link(nc.gpsimd.memset(maskT_first[:, 0], LOW))
            nc.gpsimd.tensor_scalar(maskT_first[:, 1], maskT[:, 1], 1.0, None, ALU.mult).then_inc(first_masks_ready, 1)
            ln1(Count(None, 0, 0))
            turns(pool, body)

        @block.scalar
        def _(act):
            act.wait_ge(c_loaded, 16)
            nc.scalar.activation(c_col[:, 1, :], c_col[:, 0, :], ACT.Exp, scale=-1.0).then_inc(silu_exp, 1)
            for m in range(4):
                for k in range(KT):
                    n = m * KT + k
                    act.wait_ge(wT_full, n + 1)
                    if m:
                        act.wait_ge(wT_split, 2 * (n - KT + 1))
                        act.wait_ge(wb_full, m)
                    nc.scalar.activation(wT[:, k, :], ps[:, k, :], ACT.Copy).then_inc(wT_copied, 1)

            def body(s):
                t = s + 1
                for b in range(2):
                    i = s * 2 + b
                    if (i - 1).within(0, NB):
                        need(act, pv_done, i * 8)
                        nc.scalar.activation(heads_sb[:, 1], heads_ps[1], ACT.Copy).then_inc(heads_copied, 1)
                    if b == 0 and t.within(0, NS):
                        for n in range(2):
                            need(act, xT_full, t * 2 + (n + 1))
                            bank = misc_ps[USES.index(("xT", 0, n)) % 2].rearrange("p (k t) -> p k t", k=2)
                            nc.scalar.activation(hT_hi[:, 2 * n:2 * n + 2, :], bank, ACT.Copy).then_inc(hT_hi_ready, 1)
                    if (i - 1).within(0, NB):
                        need(act, attnT_full, i)
                        bank = misc_ps[USES.index(("attnT", b, 0)) % 2].rearrange("p (k t) -> p k t", k=KT)
                        nc.scalar.activation(attnT_hi[:], bank, ACT.Copy).then_inc(attnT_hi_ready, 1)
                    if b == 0 and t.within(0, NS):
                        for g in range(4):
                            need(act, qk_full, t * 4 + (g + 1))
                            need(act, parts_stored[g % 2], t * 96 + 48 * (g // 2))
                            bank = misc_ps[USES.index(("qk", 0, g)) % 2].rearrange("p (m t) -> p m t", m=2)
                            for m in range(2):
                                mt = 2 * (g % 2) + m
                                nc.scalar.activation(parts[:, g % 2, 0, m], bank[:, m], ACT.Identity,
                                                     bias=qk_bias[:, g // 2, mt:mt + 1]).then_inc(qk_hi_ready, 1)
                    if i.within(0, NB):
                        for u in range(NPAIR):
                            need(act, st_full, i * NPAIR + (u + 1))
                            nc.scalar.activation(probs[:, u % RING], st_ps[u % 2], ACT.Exp).then_inc(exp_done, 1)
                            if u == 11:
                                need(act, pv_done, i * 8 + 4)
                                nc.scalar.activation(heads_sb[:, 0], heads_ps[0], ACT.Copy).then_inc(heads_copied, 1)
                    if (i + 1).within(0, NB):
                        need(act, mT_full, i + 2)
                        bank = misc_ps[USES.index(("mT", b, 0)) % 2]
                        nc.scalar.activation(mT[:, 0, :], bank[0:H, 0:W], ACT.Copy, scale=-1.0).then_inc(mT_hi_ready, 1)

            turns(act, body)

        @block.vector
        def _(dve):
            done = [0]

            def link(ins):
                done[0] += 1
                ins.then_inc(setup_chain, 1)
                dve.wait_ge(setup_chain, done[0])

            dve.wait_ge(silu_exp, 1)
            link(nc.vector.tensor_scalar(c_col[:, 2, :], c_col[:, 1, :], 1.0, None, ALU.add))
            link(nc.vector.reciprocal(c_col[:, 3, :], c_col[:, 2, :]))
            link(nc.vector.tensor_tensor(c_col[:, 2, :], c_col[:, 3, :], c_col[:, 0, :], ALU.mult))
            nc.vector.tensor_copy(silu_bc, c_col[:, 2, :].unsqueeze(2).to_broadcast([128, KT, 128])).then_inc(silu_ready, 1)
            dve.wait_ge(mod_cols_full, 1)
            link(nc.vector.tensor_copy(cols[:].rearrange("p a k -> p (a k)"), misc_ps[0][:, 0:3 * KT]))
            link(nc.vector.tensor_scalar(w_scale[:, 0], cols[:, 1], 1.0, None, ALU.add))
            link(nc.vector.tensor_scalar(w_scale[:, 1], w_scale[:, 0], SCALE, None, ALU.mult))

            def gate(dst, g, t0, t1):
                link(nc.vector.tensor_scalar(t0, g, -1.0, None, ALU.mult))
                link(nc.vector.tensor_tensor(t0, t0, g, ALU.max))
                link(nc.vector.tensor_scalar(t0, t0, 0.25, None, ALU.max))
                link(nc.vector.tensor_scalar(t1, g, 0.0, 2.0, ALU.is_ge, ALU.mult))
                link(nc.vector.tensor_scalar(t1, t1, -1.0, None, ALU.add))
                link(nc.vector.tensor_tensor(dst, t0, t1, ALU.mult))

            gate(cols[:, 2], cols[:, 2], g_tmp[:, 0], g_tmp[:, 1])
            nc.vector.tensor_copy(sa_bc, cols[:, 0, :].unsqueeze(2).to_broadcast([128, KT, 128])).then_inc(mod_ready, 1)
            dve.wait_ge(mod_rows_full, 1)
            link(nc.vector.tensor_scalar(cb1_row[:], ps[:, 4, :], 1.0, None, ALU.add))
            link(nc.vector.tensor_copy(sb_row[:], ps[:, 5, :]))
            link(nc.vector.tensor_copy(gb_row[:], misc_ps[1]))
            gate(gb_row[:], gb_row[:], h2[:, 1, :], attn[:])
            dve.wait_ge(w_loaded["o"], 16)
            for k in range(KT):
                ins = nc.vector.tensor_scalar(w_nat["o"][:, k, :], w_nat["o"][:, k, :], cols[:, 2, k:k + 1], None, ALU.mult)
            ins.then_inc(rows_ready, 1)
            for m, name in enumerate(MATS):
                for k in range(KT):
                    dve.wait_ge(wT_copied, m * KT + k + 1)
                    scale = 1.0 if name == "o" else w_scale[:, int(name == "q"), k:k + 1]
                    nc.vector.tensor_scalar(w_hi[name][:, k, :], wT[:, k, :], scale, None, ALU.mult).then_inc(wT_split, 1)
                    dve.wait_ge(wT_split, 2 * (m * KT + k) + 1)
                    nc.vector.scalar_tensor_tensor(w_lo[name][:, k, :], wT[:, k, :], scale,
                                                   w_hi[name][:, k, :].bitcast(fp32), ALU.mult, ALU.subtract).then_inc(wT_split, 1)
                if name == "v":
                    dve.wait_ge(wb_full, 1)
                    link(nc.vector.tensor_copy(vb_row[:], ps[:, 4, :]))
                if name == "q":
                    dve.wait_ge(wb_full, 2)
                    link(nc.vector.tensor_scalar(qk_bias[:, 0], ps[:, 5, 0:KT], SCALE, None, ALU.mult))
                if name == "k":
                    dve.wait_ge(wb_full, 3)
                    link(nc.vector.tensor_copy(qk_bias[:, 1], misc_ps[1][:, 0:KT]))
            dve.wait_ge(mod_rows_full, 1)
            link(nc.vector.memset(k_stack[96:128, :, :], 1.0))
            link(nc.vector.memset(k_stack[0:KROWS, :, 0:W], 0.0))
            link(nc.vector.memset(ps[:, 4, :], 0.0))
            nc.vector.memset(ps[:, 5, :], 0.0).then_inc(setup_done, 1)

            def ln1(t):
                p = t.parity
                need(dve, x_loaded[p], (t - p).half() * 16 + 16)
                for b in range(2):
                    nc.vector.bn_stats(stats[:, b, :], x_in[:, p, b, :]).then_inc(ln1_stats, 1)
                need(dve, ln1_stats, t * 2 + 2, apart=True)
                for b in range(2):
                    nc.vector.bn_aggr(mv[:, b, :], stats[:, b, :]).then_inc(ln1_mv, 1)

            def ln1_apply(t):
                p = t.parity
                need(dve, ln1_rstd, t + 1)
                for b in range(2):
                    nc.vector.tensor_scalar(x_in[:, p, b, :], x_in[:, p, b, :], mv[:, b, 0:1], rstd[:, b:b + 1],
                                            ALU.subtract, ALU.mult).then_inc(xhat_ready, 1)

            def divide(s, b, half, i):
                n = i * 2 + (half + 1)
                need(dve, headsT_full, n)
                bank = misc_ps[USES.index(("headsT", b, half)) % 2].rearrange("p (h e) -> p h e", e=32)
                den = r_den[:, half * 16:(half + 1) * 16]
                nc.vector.reciprocal(den, bank[:, :, DK]).then_inc(den_ready, 1)
                need(dve, den_ready, n)
                nc.vector.tensor_tensor(attn[:, half * 256:(half + 1) * 256].rearrange("p (h e) -> p h e", e=DK),
                                        bank[:, :, 0:DK], den.unsqueeze(2).to_broadcast([128, 16, DK]),
                                        ALU.mult).then_inc(attn_ready, 1)

            def body(s):
                t = s + 1
                for b in range(2):
                    i = s * 2 + b
                    tail = (i - 1).within(0, NB)
                    hb = (b + 1) % 2
                    if tail:
                        divide(s, b, 1, i - 1)
                    if b == 0 and t.within(0, NS):
                        for n in range(2):
                            need(dve, hT_hi_ready, t * 2 + (n + 1))
                            bank = misc_ps[USES.index(("xT", 0, n)) % 2].rearrange("p (k t) -> p k t", k=2)
                            nc.vector.tensor_tensor(hT_lo[:, 2 * n:2 * n + 2, :], bank,
                                                    hT_hi[:, 2 * n:2 * n + 2, :].bitcast(fp32), ALU.subtract).then_inc(hT_ready, 1)
                    if b == 1 and t.within(0, NS):
                        values(s, 0)
                    if tail:
                        need(dve, attnT_hi_ready, i)
                        bank = misc_ps[USES.index(("attnT", b, 0)) % 2].rearrange("p (k t) -> p k t", k=KT)
                        nc.vector.tensor_tensor(attnT_lo[:], bank, attnT_hi[:].bitcast(fp32), ALU.subtract).then_inc(attnT_ready, 1)
                    if b == 0 and t.within(0, NS):
                        qk_rest(s, 0)
                        qk_rest(s, 1)
                    if b == 1 and t.within(0, NS):
                        values(s, 1)
                    if tail:
                        need(dve, y_full, i)
                        need(dve, x1_loaded[hb], (s if b else s - 1) * 16 + 16)
                        nc.vector.tensor_tensor(x1[:, hb], misc_ps[USES.index(("y", b, 0)) % 2], x1[:, hb], ALU.add).then_inc(x1_ready, 1)
                        need(dve, x1_ready, i)
                        nc.vector.bn_stats(stats[:, 2, :], x1[:, hb]).then_inc(ln2_stats, 1)
                        need(dve, ln2_stats, i, apart=True)
                        nc.vector.bn_aggr(mv[:, 2, :], stats[:, 2, :]).then_inc(ln2_mv, 1)
                    if b == 0 and t.within(0, NS):
                        qk_rest(s, 2)
                        qk_rest(s, 3)
                    if b == 1 and (s + 2).within(0, NS):
                        ln1(s + 2)
                    if tail:
                        need(dve, ln2_rstd, i)
                        nc.vector.tensor_scalar(h2[:, hb], x1[:, hb], mv[:, 2, 0:1], rstd[:, 2:3],
                                                ALU.subtract, ALU.mult).then_inc(x1hat_ready, 1)
                    if b == 1 and (s + 2).within(0, NS):
                        ln1_apply(s + 2)
                    if (i + 1).within(0, NB):
                        for u in range(NSG):
                            need(dve, s_full, (i + 1) * NSG + (u + 1))
                            n = min(SG, H - u * SG)
                            nc.vector.tensor_reduce(row_max[:, u * SG:u * SG + n], s_ps[u % 2][:, 0:n, :], AX, ALU.max).then_inc(max_done, 1)
                    if tail:
                        need(dve, h2_ready, i)
                        nc.vector.tensor_reduce(h2_max[:, bass.ds((i - 1).value(), 1)], h2[:, hb], AX, ALU.max,
                                                apply_absolute_value=True).then_inc(h2_max_done, 1)
                    if i.within(0, NB):
                        divide(s, b, 0, i)
                    if (i + 1).within(0, NB):
                        need(dve, mT_hi_ready, i + 2)
                        bank = misc_ps[USES.index(("mT", b, 0)) % 2]
                        nc.vector.scalar_tensor_tensor(mT[:, 1, :], bank[0:H, 0:W], -1.0, mT[:, 0, :],
                                                       ALU.mult, ALU.subtract).then_inc(mT_ready, 1)

            def values(s, n):
                t = s + 1
                need(dve, v_full, t * 2 + (n + 1))
                slots = [1 + 2 * t.parity + n] + ([0] if t.parity and n else [])
                for at in slots:
                    ins = nc.vector.tensor_tensor(v_tok[:, at, :, 0:DK],
                                                  misc_ps[USES.index(("v", 1, n)) % 2].rearrange("p (h e) -> p h e", e=DK),
                                                  vb_row[:].rearrange("p (h e) -> p h e", e=DK), ALU.add)
                ins.then_inc(v_ready, 1)

            def qk_rest(s, g):
                t = s + 1
                need(dve, qk_hi_ready, t * 8 + (2 * g + 2))
                need(dve, qk_lo_ready, t * 4 + g)
                bank = misc_ps[USES.index(("qk", 0, g)) % 2].rearrange("p (m t) -> p m t", m=2)
                for m in range(2):
                    mt = 2 * (g % 2) + m
                    ins = nc.vector.scalar_tensor_tensor(rest[:, m], bank[:, m], qk_bias[:, g // 2, mt:mt + 1],
                                                         parts[:, g % 2, 0, m], ALU.add, ALU.subtract)
                ins.then_inc(qk_rest_ready, 1)

            ln1(Count(None, 0, 0))
            ln1_apply(Count(None, 0, 0))
            turns(dve, body)

        @block.tensor
        def _(pe):
            pe.wait_ge(silu_ready, 1)
            pe.wait_ge(wmod_loaded, 96)
            for a in range(3):
                for k in range(KT):
                    for kk in range(KT):
                        ins = nc.tensor.matmul(misc_ps[0][:, a * KT + k:a * KT + k + 1],
                                               wmod_sb[:, kk, a * D + k * 128:a * D + (k + 1) * 128],
                                               c_col[:, 2, kk:kk + 1], start=(kk == 0), stop=(kk == KT - 1))
            ins.then_inc(mod_cols_full, 1)
            for a, bank in ((3, ps[:, 5, :]), (4, ps[:, 4, :]), (5, misc_ps[1])):
                for kk in range(KT):
                    ins = nc.tensor.matmul(bank, silu_bc[:, kk, :], wmod_sb[:, kk, a * D:(a + 1) * D],
                                           start=(kk == 0), stop=(kk == KT - 1))
            ins.then_inc(mod_rows_full, 1)
            pe.wait_ge(consts_ready, 1)
            pe.wait_ge(rows_ready, 1)
            for m, name in enumerate(MATS):
                pe.wait_ge(w_loaded[name], 16)
                for k in range(KT):
                    if m:
                        pe.wait_ge(wT_copied, (m - 1) * KT + k + 1)
                    for o in range(KT):
                        ins = nc.tensor.transpose(ps[:, k, o * 128:(o + 1) * 128],
                                                  w_nat[name][:, o, k * 128:(k + 1) * 128], ident_f[:])
                    ins.then_inc(wT_full, 1)
                pe.wait_ge(wT_copied, (m + 1) * KT)
                if name == "v":
                    for k in range(KT):
                        ins = nc.tensor.matmul(ps[:, 4, :], sa_bc[:, k, :], wT[:, k, :], start=(k == 0), stop=(k == KT - 1))
                    ins.then_inc(wb_full, 1)
                elif name in "qk":
                    bank = ps[:, 5, :] if name == "q" else misc_ps[1]
                    for o in range(KT):
                        for k in range(KT):
                            ins = nc.tensor.matmul(bank[:, o:o + 1], wT[:, k, o * 128:(o + 1) * 128],
                                                   cols[:, 0, k:k + 1], start=(k == 0), stop=(k == KT - 1))
                    ins.then_inc(wb_full, 1)
            pe.wait_ge(setup_done, 1)
            pe.wait_ge(wT_split, 2 * 4 * KT)
            pe.wait_ge(first_masks_ready, 1)

            def heads_to_tokens(s, b, half, i):
                bank = misc_bank(pe, s, ("headsT", b, half))
                need(pe, heads_copied, i * 2 + (half + 1))
                for g in range(4):
                    ins = nc.tensor.transpose(bank[:, g * 128:(g + 1) * 128], heads_sb[:, half, g, :], ident_f[:])
                ins.then_inc(headsT_full, 1)

            def x_to_features(s, n):
                t = s + 1
                bank = misc_bank(pe, s, ("xT", 0, n)).rearrange("p (k t) -> p k t", k=2)
                need(pe, xhat_ready, t * 2 + 2)
                for k in range(2):
                    for b in range(2):
                        kk = 2 * n + k
                        ins = nc.tensor.transpose(bank[:, k, b * W:(b + 1) * W],
                                                  x_in[:, t.parity, b, kk * 128:(kk + 1) * 128], ident_f[:])
                ins.then_inc(xT_full, 1)

            def project_qk(s, g):
                t = s + 1
                name = "q" if g < 2 else "k"
                bank = misc_bank(pe, s, ("qk", 0, g)).rearrange("p (m t) -> p m t", m=2)
                need(pe, hT_ready, t * 2 + 2)
                for m in range(2):
                    o = (2 * (g % 2) + m) * 128
                    pairs = [(w, h, k) for k in range(KT) for w, h in ((w_hi, hT_hi), (w_hi, hT_lo), (w_lo, hT_hi))]
                    for n, (w, h, k) in enumerate(pairs):
                        ins = nc.tensor.matmul(bank[:, m], w[name][:, k, o:o + 128], h[:, k, :],
                                               start=(n == 0), stop=(n == len(pairs) - 1))
                ins.then_inc(qk_full, 1)

            def project_v(s, n):
                bank = misc_bank(pe, s, ("v", 1, n))
                pairs = [(w, h, k) for k in range(KT) for h, w in ((hT_hi, w_hi), (hT_hi, w_lo), (hT_lo, w_hi))]
                for m, (w, h, k) in enumerate(pairs):
                    ins = nc.tensor.matmul(bank, h[:, k, n * W:(n + 1) * W], w["v"][:, k, :],
                                           start=(m == 0), stop=(m == len(pairs) - 1))
                ins.then_inc(v_full, 1)

            def attn_to_features(s, b, i):
                bank = misc_bank(pe, s, ("attnT", b, 0)).rearrange("p (k t) -> p k t", k=KT)
                need(pe, attn_ready, i * 2 + 2)
                for k in range(KT):
                    ins = nc.tensor.transpose(bank[:, k], attn[:, k * 128:(k + 1) * 128], ident_f[:])
                ins.then_inc(attnT_full, 1)

            def project_out(s, b, i):
                bank = misc_bank(pe, s, ("y", b, 0))
                need(pe, attnT_ready, i + 1)
                pairs = [(w, h, k) for k in range(KT) for h, w in ((attnT_hi, w_hi), (attnT_hi, w_lo), (attnT_lo, w_hi))]
                for m, (w, h, k) in enumerate(pairs):
                    ins = nc.tensor.matmul(bank, h[:, k, :], w["o"][:, k, :], start=(m == 0), stop=(m == len(pairs) - 1))
                ins.then_inc(y_full, 1)

            def scores(s, b, u, j):
                jb = (b + 1) % 2
                js = s if b == 0 else s + 1
                first = j.k is None and j.b == 0
                if u == 0:
                    need(pe, q_loaded, js * 96 + 96)
                    need(pe, k_loaded[jb], js * 96 + 96)
                    if jb == 0 and js.parity == 0:
                        need(pe, k_carry_loaded, js.half() * 96)
                need(pe, max_done, j * NSG + max(u - 1, 0))
                n = min(SG, H - u * SG)
                bank = s_ps[u % 2]
                nc.tensor.matmul(bank[:, 0:n, :], ident_b[:],
                                 (mask_first if first else mask[:]).unsqueeze(1).to_broadcast([128, n, SK]),
                                 start=True, stop=False, skip_group_check=True)
                for h in range(n):
                    for g in range(4):
                        at = k_at(js, jb) + 32 * g
                        ins = nc.tensor.matmul(bank[32 * g:32 * g + 32, h, :],
                                               q_stack[0:KROWS, js.parity, u * SG + h, jb * W + 32 * g:jb * W + 32 * g + 32],
                                               k_stack[0:KROWS, u * SG + h, at:at + SK],
                                               start=False, stop=True, skip_group_check=True)
                ins.then_inc(s_full, 1)

            def scores_transposed(s, b, u, i):
                if u == 0:
                    need(pe, m_loaded, i * 32 + 32)
                need(pe, exp_done, i * NPAIR + (u - 1))
                m = maskT_first if i.k is None and i.b == 0 else maskT[:]
                nc.tensor.matmul(st_ps[u % 2].rearrange("p (h f) t -> p h (f t)", h=2), ident_b[:],
                                 m.rearrange("p f t -> p (f t)").unsqueeze(1).to_broadcast([128, 2, 2 * W]),
                                 start=True, stop=False, skip_group_check=True)
                for h in range(2):
                    for f in range(2):
                        at = k_at(s, b) + f * W
                        ins = nc.tensor.matmul(st_ps[u % 2][:, 2 * h + f],
                                               k_stack[0:KROWS + 2, 2 * u + h, at:at + W],
                                               q_stack[0:KROWS + 2, s.parity, 2 * u + h, b * W:(b + 1) * W],
                                               start=False, stop=True, skip_group_check=True)
                ins.then_inc(st_full, 1)

            def weigh_values(s, b, g, i):
                if g == 0:
                    need(pe, v_ready, i + 1)
                if g % 4 == 0:
                    need(pe, heads_copied, i * 2 + (g // 4 - 1))
                need(pe, exp_done, i * NPAIR + (2 * g + 2))
                for f in range(2):
                    for q in range(4):
                        h = 4 * g + q
                        ins = nc.tensor.matmul(heads_ps[g // 4][32 * q:32 * q + HR, g % 4, :],
                                               v_tok[:, 2 * s.parity + b + f, h, :],
                                               probs[:, (h // 2) % RING, 2 * (h % 2) + f, :],
                                               start=(f == 0), stop=(f == 1), skip_group_check=True)
                ins.then_inc(pv_done, 1)

            def body(s):
                t = s + 1
                for b in range(2):
                    i = s * 2 + b
                    tail, attend, score = (i - 1).within(0, NB), i.within(0, NB), (i + 1).within(0, NB)
                    proj = t.within(0, NS)
                    if tail:
                        heads_to_tokens(s, b, 1, i - 1)
                    if proj and b == 0:
                        x_to_features(s, 0)
                        x_to_features(s, 1)
                    if proj and b == 1:
                        project_v(s, 0)
                    if tail:
                        attn_to_features(s, b, i - 1)
                    if proj and b == 0:
                        project_qk(s, 0)
                        project_qk(s, 1)
                    if proj and b == 1:
                        project_v(s, 1)
                    if tail:
                        project_out(s, b, i - 1)
                    if proj and b == 0:
                        project_qk(s, 2)
                        project_qk(s, 3)
                    for u in range(NPAIR):
                        if attend:
                            scores_transposed(s, b, u, i)
                        if score and u < NSG:
                            scores(s, b, u, i + 1)
                        if attend and u % 2 and u >= 3:
                            weigh_values(s, b, (u - 3) // 2, i)
                        if attend and u == 13:
                            heads_to_tokens(s, b, 0, i)
                    if score:
                        bank = misc_bank(pe, s, ("mT", b, 0))
                        need(pe, max_done, (i + 2) * NSG)
                        nc.tensor.transpose(bank[0:H, 0:W], row_max[:], ident_f[:]).then_inc(mT_full, 1)
                    if attend:
                        weigh_values(s, b, 7, i)

            turns(pe, body)

        first_phase.close()
        block = ctx.enter_context(nc.Block())
        taken = [0]

        def carve(elems, dt, pattern=None, **sizes):
            size = elems * (2 if dt == fp32 or dt == u32 else 1)
            piece = stacks[:, taken[0]:taken[0] + size]
            taken[0] += size
            piece = piece if dt == bf16 else piece.bitcast(dt)
            return piece.rearrange(pattern, **sizes) if pattern else piece

        wf = carve(KT * D, fp32)
        wf_unit = carve(KT * D, fp32)
        wf_magic = carve(KT * D, fp32)
        wf_q = carve(KT * D, bf16, "p (k d) -> p k d", k=KT)
        wf_qT = carve(KT * D, bf16, "p (k d) -> p k d", k=KT)
        bias_all = carve(D, fp32)
        bias_part = carve(3 * D, bf16, "p (a d) -> p a d", a=3)
        bias_rows = carve(D, bf16)
        ones_rows = carve(128, bf16)
        ratio = carve(16, fp32)
        h2_in = carve(2 * D, fp32, "p (r d) -> p r d", r=2)
        x1_in = carve(2 * D, fp32, "p (r d) -> p r d", r=2)
        unit = carve(2 * D, fp32, "p (r d) -> p r d", r=2)
        magic = carve(2 * D, fp32, "p (r d) -> p r d", r=2)
        rounded = carve(2 * D, fp32, "p (r d) -> p r d", r=2)
        hq = carve(2 * D, bf16, "p (r d) -> p r d", r=2)
        hqT = carve(2 * KT * W, bf16, "p (r k t) -> p r k t", r=2, k=KT)
        result = carve(2 * D, fp32, "p (r d) -> p r d", r=2)

        wf_loaded = sem("wf_loaded")
        bias_loaded = sem("bias_loaded")
        amax_own = sem("amax_own")
        amax_ready = sem("amax_ready")
        prep = sem("prep")
        scales_ready = sem("scales_ready")
        wf_ready = sem("wf_ready")
        wfT_full = sem("wfT_full")
        wfT_ready = sem("wfT_ready")
        bias_ready = sem("bias_ready")
        h2_loaded = [sem("h2_loaded_0"), sem("h2_loaded_1")]
        x1_back = [sem("x1_back_0"), sem("x1_back_1")]
        unit_ready = sem("unit_ready")
        power_ready = sem("power_ready")
        magic_ready = sem("magic_ready")
        rounded_ready = sem("rounded_ready")
        hq_ready = sem("hq_ready")
        hqT_full = sem("hqT_full")
        hqT_ready = sem("hqT_ready")
        z_full = sem("z_full")
        z_scaled = sem("z_scaled")
        result_ready = sem("result_ready")
        result_stored = [sem("result_stored_0"), sem("result_stored_1")]

        EXPONENT, SMALLEST, MAGIC = 0x7F800000, 2.0 ** -6, 1.5 * 2.0 ** 20

        def rounds(eng, body):
            for n in range(4):
                body(Count(None, 0, n))
            with eng.Fori(0, (NB - 4) // 2) as k:
                body(Count(k, 2, 4))
                body(Count(k, 2, 5))
            body(Count(None, 0, NB))
            body(Count(None, 0, NB + 1))

        hqT_ps = [ps[:, r, 0:KT * W // 2].bitcast(bf16).rearrange("p (k t) -> p k t", k=KT) for r in range(2)]
        z_ps = [ps[:, 2 + r, :] for r in range(2)]
        wfT_ps = [ps[:, 4 + k, 0:D // 2].bitcast(bf16) for k in range(KT)]

        @block.sync
        def _(sp):
            sp.dma_start(wf.rearrange("p (k d) -> p k d", k=KT), Wf.rearrange("(k p) d -> p k d", p=128)).then_inc(wf_loaded, 16)
            sp.dma_start(bias_all, bias.unsqueeze(0).to_broadcast([128, D])).then_inc(bias_loaded, 16)

            def load_h2(n):
                p = n.parity
                need(sp, unit_ready, n - 1)
                sp.dma_start(h2_in[:, p], h2_dram[bass.ds(n.value(), 1)].rearrange("a p d -> p (a d)")).then_inc(h2_loaded[p], 16)

            def load_x1(n):
                p = n.parity
                need(sp, result_ready, n - 1)
                sp.dma_start(x1_in[:, p], x1_dram[bass.ds(n.value(), 1)].rearrange("a p d -> p (a d)")).then_inc(x1_back[p], 16)

            def store(n):
                need(sp, result_ready, n + 1)
                sp.dma_start(ob[bass.ds(n.value(), 1)].rearrange("a p d -> p (a d)"), result[:, n.parity]).then_inc(result_stored[n.parity], 16)

            def body(n):
                if n.within(0, NB):
                    load_h2(n)
                if (n - 2).within(0, NB):
                    store(n - 2)
                if n.within(0, NB):
                    load_x1(n)

            rounds(sp, body)
            for r in range(2):
                sp.wait_ge(result_stored[r], 16 * (NB // 2))

        @block.gpsimd
        def _(pool):
            pool.wait_ge(amax_own, 2)
            nc.gpsimd.partition_all_reduce(q8[:, 2:4], q8[:, 0:2], 128, bass.bass_isa.ReduceOp.max).then_inc(amax_ready, 1)

            def round_up(n):
                p = n.parity
                need(pool, magic_ready, n + 1)
                nc.gpsimd.tensor_tensor(rounded[:, p], unit[:, p], magic[:, p], ALU.add).then_inc(rounded_ready, 1)

            def finish(n):
                p = n.parity
                need(pool, z_scaled, n + 1)
                need(pool, x1_back[p], (n - p).half() * 16 + 16)
                nc.gpsimd.tensor_tensor(result[:, p], result[:, p], x1_in[:, p], ALU.add).then_inc(result_ready, 1)

            def body(n):
                if n.within(0, NB):
                    round_up(n)
                if (n - 1).within(0, NB):
                    finish(n - 1)

            rounds(pool, body)

        @block.scalar
        def _(act):
            act.wait_ge(scales_ready, 1)

            def units(n):
                p = n.parity
                need(act, h2_loaded[p], (n - p).half() * 16 + 16)
                need(act, rounded_ready, n - 1)
                nc.scalar.activation(unit[:, p], h2_in[:, p], ACT.Copy, scale=q8[:, 6:7]).then_inc(unit_ready, 1)

            def turn_over(n):
                need(act, hqT_full, n + 1)
                nc.scalar.activation(hqT[:, n.parity], hqT_ps[n.parity], ACT.Copy).then_inc(hqT_ready, 1)

            for k in range(KT):
                act.wait_ge(wfT_full, k + 1)
                nc.scalar.activation(wf_qT[:, k], wfT_ps[k], ACT.Copy).then_inc(wfT_ready, 1)

            def body(n):
                if n.within(0, NB):
                    units(n)
                if (n - 1).within(0, NB):
                    turn_over(n - 1)

            rounds(act, body)

        @block.vector
        def _(dve):
            done = [0]

            def link(ins):
                done[0] += 1
                ins.then_inc(prep, 1)
                dve.wait_ge(prep, done[0])

            nc.vector.tensor_reduce(q8[:, 0:1], h2_max[:], AX, ALU.max).then_inc(amax_own, 1)
            dve.wait_ge(wf_loaded, 16)
            nc.vector.tensor_reduce(q8[:, 1:2], wf, AX, ALU.max, apply_absolute_value=True).then_inc(amax_own, 1)
            dve.wait_ge(amax_ready, 1)
            link(nc.vector.tensor_tensor(q8[:, 3:4], q8[:, 3:4], q8[:, 2:3], ALU.max))
            link(nc.vector.tensor_scalar(q8[:, 4:6], q8[:, 2:4], 1.0 / QMAX, None, ALU.mult))
            link(nc.vector.reciprocal(q8[:, 6:8], q8[:, 4:6]))
            link(nc.vector.tensor_tensor(ratio[:, 0:1], q8[:, 4:5], q8[:, 5:6], ALU.mult))
            nc.vector.tensor_tensor(ratio[:, 1:2], q8[:, 6:7], q8[:, 7:8], ALU.mult).then_inc(scales_ready, 1)
            dve.wait_ge(scales_ready, 1)
            link(nc.vector.tensor_scalar(wf_unit, wf, q8[:, 7:8], None, ALU.mult))
            link(nc.vector.tensor_scalar(wf_magic.bitcast(u32), wf_unit.bitcast(u32), EXPONENT, None, ALU.bitwise_and))
            link(nc.vector.tensor_scalar(wf_magic, wf_magic, SMALLEST, MAGIC, ALU.max, ALU.mult))
            link(nc.vector.tensor_tensor(wf_unit, wf_unit, wf_magic, ALU.add))
            nc.vector.tensor_tensor(wf_q.rearrange("p k d -> p (k d)"), wf_unit, wf_magic, ALU.subtract).then_inc(wf_ready, 1)
            link(nc.vector.tensor_scalar(gb_row[:], gb_row[:], ratio[:, 0:1], None, ALU.mult))
            dve.wait_ge(bias_loaded, 16)
            link(nc.vector.tensor_scalar(bias_all, bias_all, ratio[:, 1:2], None, ALU.mult))
            for a in range(3):
                link(nc.vector.tensor_copy(bias_part[:, a], bias_all))
                if a < 2:
                    link(nc.vector.tensor_tensor(bias_all, bias_all, bias_part[:, a], ALU.subtract))
            link(nc.vector.memset(bias_rows, 0.0))
            link(nc.vector.memset(ones_rows, 1.0))
            for a in range(3):
                ins = nc.vector.tensor_copy(bias_rows[32 * a:32 * a + 1], bias_part[32 * a:32 * a + 1, a])
            ins.then_inc(bias_ready, 1)

            def powers(n):
                p = n.parity
                need(dve, unit_ready, n + 1)
                nc.vector.tensor_scalar(magic[:, p].bitcast(u32), unit[:, p].bitcast(u32), EXPONENT, None, ALU.bitwise_and).then_inc(power_ready, 1)
                need(dve, power_ready, n + 1)
                nc.vector.tensor_scalar(magic[:, p], magic[:, p], SMALLEST, MAGIC, ALU.max, ALU.mult).then_inc(magic_ready, 1)

            def grid(n):
                p = n.parity
                need(dve, rounded_ready, n + 1)
                need(dve, hqT_full, n - 1)
                nc.vector.tensor_tensor(hq[:, p], rounded[:, p], magic[:, p], ALU.subtract).then_inc(hq_ready, 1)

            def scaled(n):
                p = n.parity
                need(dve, z_full, n + 1)
                need(dve, result_stored[p], (n - p).half() * 16)
                nc.vector.tensor_tensor(result[:, p], z_ps[p], gb_row[:], ALU.mult).then_inc(z_scaled, 1)

            def body(n):
                if (n - 1).within(0, NB):
                    grid(n - 1)
                if (n - 2).within(0, NB):
                    scaled(n - 2)
                if n.within(0, NB):
                    powers(n)

            rounds(dve, body)

        @block.tensor
        def _(pe):
            pe.wait_ge(wf_ready, 1)
            for k in range(KT):
                for o in range(KT):
                    ins = nc.tensor.transpose(wfT_ps[k][:, o * 128:(o + 1) * 128], wf_q[:, o, k * 128:(k + 1) * 128], ident_b[:])
                ins.then_inc(wfT_full, 1)
            pe.wait_ge(wfT_ready, KT)
            pe.wait_ge(bias_ready, 1)

            def transposed(n):
                need(pe, hq_ready, n + 1)
                need(pe, hqT_ready, n - 1)
                for k in range(KT):
                    ins = nc.tensor.transpose(hqT_ps[n.parity][:, k], hq[:, n.parity, k * 128:(k + 1) * 128], ident_b[:])
                ins.then_inc(hqT_full, 1)

            def product(n):
                need(pe, hqT_ready, n + 1)
                need(pe, z_scaled, n - 1)
                for k in range(KT):
                    nc.tensor.matmul(z_ps[n.parity], hqT[:, n.parity, k], wf_qT[:, k], start=(k == 0), stop=False)
                nc.tensor.matmul(z_ps[n.parity], ones_rows[0:96], bias_rows[0:96], start=False, stop=True).then_inc(z_full, 1)

            def body(n):
                if n.within(0, NB):
                    transposed(n)
                if (n - 1).within(0, NB):
                    product(n - 1)

            rounds(pe, body)


_INS = ['L0_attn_x', 'L0_attn_Wq', 'L0_attn_Wk', 'L0_attn_Wv', 'L0_attn_Wo', 'L0_ffn_weight', 'L0_ffn_bias', 'L0_c', 'L0_wmod']
_OUTS = [((1, 4096, 512), 'float32')]


def kernel(**inputs):
    import numpy as _np
    import concourse.bacc as _bacc
    from concourse import mybir as _mybir
    from concourse.bass_utils import run_bass_kernel_spmd as _run

    nc = _bacc.Bacc("TRN2", target_bir_lowering=False, num_devices=1)
    arrays, args = {}, []
    for name in _INS:
        a = _np.ascontiguousarray(inputs[name])
        arrays[f"in_{name}_dram"] = a
        args.append(nc.dram_tensor(f"in_{name}_dram", a.shape, _mybir.dt.from_np(a.dtype), kind="ExternalInput").ap())
    for i, (shape, dtype) in enumerate(_OUTS):
        dt = _mybir.dt.from_np(_np.dtype(dtype))
        args.append(nc.dram_tensor(f"out_{i}_dram", shape, dt, kind="ExternalOutput").ap())
    adaln_block(nc, *args)
    r = _run(nc, [arrays], core_ids=[0])
    return r.results[0]["out_0_dram"]
```

```python
import numpy as np

import concourse.bass as bass
from concourse import mybir
from contextlib import ExitStack


class Count:

    def __init__(self, k, a, b):
        self.k, self.a, self.b = k, (a if k is not None else 0), b

    def __mul__(self, m):
        return Count(self.k, self.a * m, self.b * m)

    def __add__(self, n):
        return Count(self.k, self.a, self.b + n)

    def __sub__(self, n):
        return self + (-n)

    def half(self):
        return Count(self.k, self.a // 2, self.b // 2)

    def over(self, m):
        return Count(self.k, self.a // m, self.b // m)

    @property
    def parity(self):
        return self.b % 2

    @property
    def slot(self):
        return self.b % 4

    def within(self, lo, hi):
        return True if self.k is not None else lo <= self.b < hi

    def value(self):
        return self.b if self.k is None or self.a == 0 else self.k * self.a + self.b


def need(eng, sem, count, apart=False):
    if isinstance(count, Count):
        if count.k is None and count.b <= 0:
            return
        assert count.b > 0, "a looped turn waits for something"
        eng.wait_ge(sem, count.value())
        if apart and count.k is not None:
            eng.nop(nofuse=True)
    elif count > 0:
        eng.wait_ge(sem, count)


def adaln_block(nc: bass.Bass, x, Wq, Wk, Wv, Wo, Wf, bias, c, wmod, out):
    fp32 = mybir.dt.float32
    fp32r = mybir.dt.float32r
    bf16 = mybir.dt.bfloat16
    u32 = mybir.dt.uint32
    ALU = mybir.AluOpType
    ACT = mybir.ActivationFunctionType
    AX = mybir.AxisListType.X

    T, D = x.shape[1], x.shape[2]
    H, DK = 32, D // 32
    W = 128
    KT = D // 128
    NB = T // W
    ST = 2 * W
    NS = T // ST
    SK = W + 32
    SG = 3
    NSG = (H + SG - 1) // SG
    NPAIR = H // 2
    RING = 4
    HR = DK + 1
    KROWS = 6 * DK
    EPS = 1e-5
    SCALE = 1.0 / DK ** 0.5
    QMAX = 448.0 * 0.8
    LOW = -3.0e38
    TWO_ONES = float(np.array([0x3F803F80], np.uint32).view(np.float32)[0])

    xs = x.rearrange("a (s b p) d -> (a s) p b d", b=2, p=128)
    xb = x.rearrange("a (n p) d -> (a n) p d", p=128)
    ob = out.rearrange("a (n p) d -> (a n) p d", p=128)

    ctx = ExitStack()
    with ctx:
        def sb(name, shape, dt):
            return ctx.enter_context(nc.sbuf_tensor(name, shape, dt))

        def sem(name):
            return ctx.enter_context(nc.semaphore(name))

        q_parts_dram = nc.dram_tensor("q_parts", [3, D, T], bf16, kind="Internal").ap()
        k_parts_dram = nc.dram_tensor("k_parts", [3, D, T], bf16, kind="Internal").ap()
        x1_dram = nc.dram_tensor("x1_scratch", [NB, 128, D], fp32, kind="Internal").ap()
        h2_dram = nc.dram_tensor("h2_scratch", [NB, 128, D], fp32, kind="Internal").ap()
        parts_dram = {"q": q_parts_dram, "k": k_parts_dram}

        w_hi = {n: sb(f"w{n}_hi", [128, KT, D], fp32r) for n in "qkvo"}
        w_lo = {n: sb(f"w{n}_lo", [128, KT, D], fp32r) for n in "qkvo"}
        Q_SLOTS, K_SLOTS = (0, 0, 0, 1, 1, 2), (0, 1, 2, 0, 1, 0)
        stacks = sb("stacks", [128, H * (2 * ST + W + 2 * ST)], bf16)
        q_stack = stacks[:, 0:2 * H * ST].rearrange("p (r h t) -> p r h t", r=2, h=H)
        k_stack = stacks[:, 2 * H * ST:].rearrange("p (h t) -> p h t", h=H)

        x_in = sb("x_in", [128, 2, 2, D], fp32)
        hT_hi = sb("hT_hi", [128, KT, ST], fp32r)
        hT_lo = sb("hT_lo", [128, KT, ST], fp32r)
        parts = sb("parts", [128, 2, 3, 2, ST], bf16)
        rest = sb("rest", [128, 2, ST], fp32)
        v_tok = sb("v_tok", [128, 5, H, HR], fp32)
        probs = sb("probs", [128, RING, 4, W], fp32)
        cb1_row = sb("cb1_row", [128, D], fp32)
        sb_row = sb("sb_row", [128, D], fp32)
        gb_row = sb("gb_row", [128, D], fp32)
        vb_row = sb("vb_row", [128, D], fp32)
        work = sb("work", [128, 2 * D + 2 * D], fp32)
        x1 = work[:, 0:2 * D].rearrange("p (r d) -> p r d", r=2)
        heads_sb = work[:, 2 * D:4 * D].rearrange("p (f g t) -> p f g t", f=2, g=4)
        h2 = sb("h2", [128, 2, D], fp32)
        attn = sb("attn", [128, D], fp32)
        attnT_hi = sb("attnT_hi", [128, KT, W], fp32r)
        attnT_lo = sb("attnT_lo", [128, KT, W], fp32r)
        ident_f = sb("ident_f", [128, 128], fp32)
        ident_b = sb("ident_b", [128, 128], bf16)
        mask = sb("mask", [128, SK], bf16)
        maskT = sb("maskT", [128, 2, W], bf16)
        first_masks = h2[:, 0, :].bitcast(bf16)
        mask_first = first_masks[:, 0:SK]
        maskT_first = first_masks[:, 2 * W:4 * W].rearrange("p (f t) -> p f t", f=2)
        row_max = sb("row_max", [128, H], fp32)
        r_den = sb("r_den", [128, H], fp32)
        mT = sb("mT", [H, 2, W], bf16)
        stats = sb("stats", [128, 3, 6], fp32)
        mv = sb("mv", [128, 3, 2], fp32)
        rstd = sb("rstd", [128, 3], fp32)
        m_half = sb("m_half", [128, 3], fp32)
        h2_max = sb("h2_max", [128, NB], fp32)
        cols = sb("cols", [128, 3, KT], fp32)
        c_col = sb("c_col", [128, 4, KT], fp32)
        g_tmp = sb("g_tmp", [128, 2, KT], fp32)
        w_scale = sb("w_scale", [128, 2, KT], fp32)
        qk_bias = sb("qk_bias", [128, 2, KT], fp32)
        q8 = sb("q8", [128, 8], fp32)

        ps = ctx.enter_context(nc.psum_tensor("ps", [128, 8, 512], fp32))
        st_ps = [ps[:, 0 + b, :].rearrange("p (f t) -> p f t", f=4) for b in range(2)]
        s_ps = [ps[:, 2 + b, 0:SG * SK].rearrange("p (h t) -> p h t", h=SG) for b in range(2)]
        heads_ps = [ps[:, 4 + b, :].rearrange("p (g t) -> p g t", g=4) for b in range(2)]
        misc_ps = [ps[:, 6 + b, :] for b in range(2)]

        c_loaded = sem("c_loaded")
        wmod_loaded = sem("wmod_loaded")
        w_loaded = {n: sem(f"w{n}_loaded") for n in "qkvo"}
        consts_step = sem("consts_step")
        consts_ready = sem("consts_ready")
        first_masks_ready = sem("first_masks_ready")
        silu_exp = sem("silu_exp")
        setup_chain = sem("setup_chain")
        silu_ready = sem("silu_ready")
        mod_cols_full = sem("mod_cols_full")
        mod_rows_full = sem("mod_rows_full")
        mod_ready = sem("mod_ready")
        rows_ready = sem("rows_ready")
        wT_full = sem("wT_full")
        wT_copied = sem("wT_copied")
        wT_split = sem("wT_split")
        wb_full = sem("wb_full")
        setup_done = sem("setup_done")
        x_loaded = [sem("x_loaded_even"), sem("x_loaded_odd")]
        x1_loaded = [sem("xres_loaded_0"), sem("xres_loaded_1")]
        ln1_stats = sem("ln1_stats")
        ln1_mv = sem("ln1_mv")
        ln1_eps = sem("ln1_eps")
        ln1_rstd = sem("ln1_rstd")
        xhat_ready = sem("xhat_ready")
        xT_full = sem("xT_full")
        hT_hi_ready = sem("hT_hi_ready")
        hT_ready = sem("hT_ready")
        qk_full = sem("qk_full")
        qk_hi_ready = sem("qk_hi_ready")
        qk_rest_ready = sem("qk_rest_ready")
        qk_mid_ready = sem("qk_mid_ready")
        qk_lo_ready = sem("qk_lo_ready")
        parts_stored = [sem("parts_stored_0"), sem("parts_stored_1")]
        q_loaded = sem("q_loaded")
        k_loaded = [sem("k_loaded_0"), sem("k_loaded_1")]
        k_carry_loaded = sem("k_carry_loaded")
        v_full = sem("v_full")
        v_ready = sem("v_ready")
        s_full = sem("s_full")
        max_done = sem("max_done")
        mT_full = sem("mT_full")
        mT_hi_ready = sem("mT_hi_ready")
        mT_ready = sem("mT_ready")
        m_loaded = sem("m_loaded")
        st_full = sem("st_full")
        st_masked = sem("st_masked")
        exp_done = sem("exp_done")
        pv_done = sem("pv_done")
        heads_copied = sem("heads_copied")
        headsT_full = sem("headsT_full")
        den_ready = sem("den_ready")
        attn_ready = sem("attn_ready")
        attnT_full = sem("attnT_full")
        attnT_hi_ready = sem("attnT_hi_ready")
        attnT_ready = sem("attnT_ready")
        y_full = sem("y_full")
        x1_ready = sem("x1_ready")
        ln2_stats = sem("ln2_stats")
        ln2_mv = sem("ln2_mv")
        ln2_eps = sem("ln2_eps")
        ln2_rstd = sem("ln2_rstd")
        x1hat_ready = sem("x1hat_ready")
        h2_scaled = sem("h2_scaled")
        h2_ready = sem("h2_ready")
        h2_max_done = sem("h2_max_done")
        x1_stored = [sem("x1_stored_0"), sem("x1_stored_1")]
        h2_stored = [sem("h2_stored_0"), sem("h2_stored_1")]

        USES = {("xT", 0, 0): 2, ("xT", 0, 1): 3, ("headsT", 0, 1): 6, ("qk", 0, 0): 7, ("attnT", 0, 0): 6,
                ("qk", 0, 1): 2, ("y", 0, 0): 6, ("qk", 0, 2): 3, ("qk", 0, 3): 7, ("scores", 0, 0): 2,
                ("scores", 0, 1): 3, ("headsT", 0, 0): 6, ("mT", 0, 0): 7,
                ("v", 1, 0): 2, ("headsT", 1, 1): 6, ("v", 1, 1): 3, ("attnT", 1, 0): 7, ("y", 1, 0): 6,
                ("scores", 1, 0): 2, ("scores", 1, 1): 3, ("headsT", 1, 0): 7, ("mT", 1, 0): 6}
        FREED = {"xT": hT_ready, "qk": qk_rest_ready, "v": v_ready, "headsT": attn_ready,
                 "attnT": attnT_ready, "y": x1_ready, "scores": max_done, "mT": mT_ready}

        def nth(s, use):
            kind, b, n = use
            if kind in ("xT", "v"):
                return s * 2 + (2 + n), 2 * NS
            if kind == "qk":
                return s * 4 + (4 + n), 4 * NS
            if kind == "headsT":
                return s * 4 + (2 * b + n if n == 0 else 2 * b - 1), 2 * NB
            if kind in ("attnT", "y"):
                return s * 2 + (b - 1), NB
            if kind == "scores":
                return s * (2 * NSG) + ((b + 1) * NSG + NSG - 1 - (NSG - 1 - n) % 2), NB * NSG
            return s * 2 + (b + 1), NB

        def bank_of(kind, b, n):
            return ps[:, USES[kind, b, n], :]

        def take_bank(pe, s, *use):
            order = [u for u in USES if USES[u] == USES[use]]
            pos, back = order.index(use), s
            while True:
                pos -= 1
                if pos < 0:
                    pos, back = pos + len(order), back - 1
                if back.k is None and back.b < -1:
                    break
                n, total = nth(back, order[pos])
                if n.within(0, total):
                    need(pe, FREED[order[pos][0]], n + 1)
                    break
            return bank_of(*use)

        MASKED = (2, 4, 6, 8, 10, 12, 14)

        def masked(i, u):
            return i * len(MASKED) + (MASKED.index(u) + 1)

        def turns(eng, body):
            body(Count(None, 0, -1))
            body(Count(None, 0, 0))
            with eng.Fori(0, (NS - 4) // 2) as k:
                body(Count(k, 2, 1))
                body(Count(k, 2, 2))
            for s in range(NS - 3, NS + 1):
                body(Count(None, 0, s))

        def k_at(s, b):
            return ST * s.parity + W * b

        late = stacks[:, 0:2 * 2 * KT * D].bitcast(fp32)
        wf = late[:, 0:KT * D]
        x1_in = late[:, KT * D:2 * KT * D].rearrange("p (r d) -> p r d", r=4)
        h2_in = x_in[:].rearrange("p r b d -> p (r b) d")
        bias_all = rest[:].rearrange("p m t -> p (m t)")
        wf_loaded = sem("wf_loaded")
        bias_loaded = sem("bias_loaded")
        h2_loaded = [sem(f"h2_loaded_{r}") for r in range(4)]
        x1_back = [sem(f"x1_back_{r}") for r in range(4)]
        wf_max_ready = sem("wf_max_ready")

        first_phase = ExitStack()
        block = first_phase.enter_context(nc.Block())
        wmod_sb = stacks[:, 0:2 * KT * 6 * D].bitcast(fp32).rearrange("p (k n) -> p k n", k=KT)
        wst = stacks[:, 2 * KT * 6 * D:2 * KT * 6 * D + 6 * KT * D].bitcast(fp32).rearrange(
            "p (w k d) -> p w k d", w=3, k=KT)
        w_nat = {"q": wst[:, 0], "k": wst[:, 1], "v": wst[:, 2],
                 "o": probs[:].rearrange("p r f t -> p (r f t)").rearrange("p (k d) -> p k d", k=KT)}
        wT = work[:].rearrange("p (k d) -> p k d", k=KT)
        silu_bc = attn[:].rearrange("p (k m) -> p k m", k=KT)
        sa_bc = h2[:, 0, :].rearrange("p (k m) -> p k m", k=KT)
        MATS = ("v", "q", "k", "o")

        @block.sync
        def _(sp):
            with nc.allow_non_contiguous_dma(reason="512 values, once"):
                sp.dma_start(c_col[:, 0, :], c.rearrange("a (k p) -> p (a k)", p=128)).then_inc(c_loaded, 16)
            wmod_v = wmod.rearrange("(k p) n -> p k n", p=128)
            for n in range(6):
                sp.dma_start(wmod_sb[:, :, n * D:(n + 1) * D], wmod_v[:, :, n * D:(n + 1) * D]).then_inc(wmod_loaded, 16)
            for n, w in (("v", Wv), ("q", Wq), ("k", Wk), ("o", Wo)):
                sp.dma_start(w_nat[n], w.rearrange("(k p) d -> p k d", p=128)).then_inc(w_loaded[n], 16)
            for s in range(2):
                sp.dma_start(x_in[:, s], xs[s]).then_inc(x_loaded[s], 16)
            sp.wait_ge(setup_done, 1)

            def store_parts(s, g):
                t = s + 1
                need(sp, qk_lo_ready, t * 4 + (g + 1), apart=True)
                dram = parts_dram["q" if g < 2 else "k"]
                for part in range(3):
                    rows = dram[part, (g % 2) * 2 * 128:((g % 2) * 2 + 2) * 128, :].rearrange("(m p) t -> p m t", p=128)
                    sp.dma_start(rows[:, :, bass.ds((t * ST).value(), ST)],
                                 parts[:, g % 2, part]).then_inc(parts_stored[g % 2], 16)

            def load_stack(dst, name, slots, start, n, done):
                for row, part in enumerate(slots):
                    src = parts_dram[name][part].rearrange("(h d) t -> d h t", d=DK)
                    sp.dma_start(dst[row * DK:(row + 1) * DK], src[:, :, bass.ds(start, n)]).then_inc(done, 16)

            def load_second():
                sp.wait_ge(st_full, (NS - 1) * 2 * NPAIR)
                sp.wait_ge(xT_full, 2 * NS)
                sp.wait_ge(qk_lo_ready, 4 * NS)
                sp.dma_start(wf.rearrange("p (k d) -> p k d", k=KT), Wf.rearrange("(k p) d -> p k d", p=128)).then_inc(wf_loaded, 16)
                sp.dma_start(bias_all, bias.unsqueeze(0).to_broadcast([128, D])).then_inc(bias_loaded, 16)
                for n in range(4):
                    sp.dma_start(h2_in[:, n], h2_dram[n]).then_inc(h2_loaded[n], 16)

            def body(s):
                t = s + 1
                for b in range(2):
                    i = s * 2 + b
                    if i.within(0, NB):
                        need(sp, h2_stored[b], s * 16, apart=True)
                        need(sp, x1_stored[b], s * 16, apart=True)
                        sp.dma_start(x1[:, b, :], xb[bass.ds(i.value(), 1)].rearrange("a p d -> p (a d)")
                                     ).then_inc(x1_loaded[b], 16)
                    if b == 0 and t.within(0, NS):
                        store_parts(s, 0)
                        store_parts(s, 1)
                        need(sp, parts_stored[0], t * 96 + 48, apart=True)
                        need(sp, parts_stored[1], t * 96 + 48, apart=True)
                        need(sp, st_full, s * (2 * NPAIR), apart=True)
                        load_stack(q_stack[:, t.parity], "q", Q_SLOTS, (t * ST).value(), ST, q_loaded)
                        store_parts(s, 2)
                        store_parts(s, 3)
                        need(sp, parts_stored[0], t * 96 + 96, apart=True)
                        need(sp, parts_stored[1], t * 96 + 96, apart=True)
                        load_stack(k_stack[:, :, k_at(t, 0) + W:k_at(t, 0) + 2 * W], "k", K_SLOTS,
                                   (t * ST).value(), W, k_loaded[0])
                    if b == 0 and (s + 3).within(2, NS):
                        need(sp, xT_full, t * 2 + 2, apart=True)
                        load_x(s + 3)
                    j = i + 1
                    if (i - 1).within(0, NB):
                        store_block(i - 1, (b + 1) % 2, s if b else s - 1)
                    if j.within(0, NB):
                        need(sp, mT_ready, j + 1, apart=True)
                        jb = (b + 1) % 2
                        jp = s.parity if b == 0 else t.parity
                        for part in range(2):
                            sp.dma_start(q_stack[KROWS + part:KROWS + part + 1, jp, :, jb * W:(jb + 1) * W],
                                         mT[:, part, :]).then_inc(m_loaded, 16)
                    if b == 0 and t.within(0, NS):
                        need(sp, st_full, (s * 2 + 1) * NPAIR, apart=True)
                        load_stack(k_stack[:, :, k_at(t, 1) + W:k_at(t, 1) + 2 * W], "k", K_SLOTS,
                                   (t * ST + W).value(), W, k_loaded[1])
                        if t.parity:
                            load_stack(k_stack[:, :, 0:W], "k", K_SLOTS, (t * ST + W).value(), W, k_carry_loaded)

                    if b == 0 and s.k is None and s.b == NS - 1:
                        load_second()

            def load_x(t):
                sp.dma_start(x_in[:, t.parity],
                             xs[bass.ds(t.value(), 1)].rearrange("a p b d -> p (a b) d")).then_inc(x_loaded[t.parity], 16)

            def store_block(i, b, s):
                need(sp, ln2_mv, i + 1, apart=True)
                need(sp, x1hat_ready, i + 1, apart=True)
                sp.dma_start(x1_dram[bass.ds(i.value(), 1)].rearrange("a p d -> p (a d)"), x1[:, b, :]).then_inc(x1_stored[b], 16)
                need(sp, h2_ready, i + 1, apart=True)
                sp.dma_start(h2_dram[bass.ds(i.value(), 1)].rearrange("a p d -> p (a d)"), h2[:, b, :]).then_inc(h2_stored[b], 16)

            turns(sp, body)
            for b in range(2):
                sp.wait_ge(x1_stored[b], 16 * (NB // 2))
                sp.wait_ge(h2_stored[b], 16 * (NB // 2))

        @block.gpsimd
        def _(pool):
            done = [0]

            def link(ins):
                done[0] += 1
                ins.then_inc(consts_step, 1)
                pool.wait_ge(consts_step, done[0])

            link(nc.gpsimd.memset(ident_f[:], 1.0))
            link(nc.gpsimd.affine_select(out=ident_f[:], in_=ident_f[:], compare_op=ALU.is_equal, fill=0.0, base=0,
                                         pattern=[[-1, 128]], channel_multiplier=1))
            link(nc.gpsimd.tensor_scalar(ident_b[:], ident_f[:], 1.0, None, ALU.mult))
            link(nc.gpsimd.memset(m_half[:], -0.5))
            link(nc.gpsimd.memset(mask[:], 0.0))
            for g in range(4):
                rows = mask[32 * g:32 * g + 32, :]
                link(nc.gpsimd.affine_select(out=rows, in_=rows, compare_op=ALU.is_ge, fill=LOW, base=0,
                                             pattern=[[1, SK]], channel_multiplier=-1))
                link(nc.gpsimd.affine_select(out=rows, in_=rows, compare_op=ALU.is_ge, fill=LOW, base=W,
                                             pattern=[[-1, SK]], channel_multiplier=1))
            link(nc.gpsimd.memset(maskT[:], 0.0))
            link(nc.gpsimd.affine_select(out=maskT[:, 0], in_=maskT[:, 0], compare_op=ALU.is_ge, fill=LOW, base=0,
                                         pattern=[[-1, W]], channel_multiplier=1))
            link(nc.gpsimd.affine_select(out=maskT[:, 1], in_=maskT[:, 1], compare_op=ALU.is_ge, fill=LOW, base=0,
                                         pattern=[[1, W]], channel_multiplier=-1))
            nc.gpsimd.memset(v_tok[:], 1.0).then_inc(consts_ready, 1)

            def inv_std(at, mv_ready, eps_added, ready, n, first, last):
                need(pool, mv_ready, n, apart=True)
                nc.gpsimd.tensor_scalar(rstd[:, first:last], mv[:, first:last, 1], EPS, None, ALU.add).then_inc(eps_added, 1)
                need(pool, eps_added, at, apart=True)
                nc.gpsimd.tensor_tensor(rstd[:, first:last], rstd[:, first:last], m_half[:, first:last],
                                        ALU.pow).then_inc(ready, 1)

            def ln1(t):
                inv_std(t + 1, ln1_mv, ln1_eps, ln1_rstd, t * 2 + 2, 0, 2)

            def body(s):
                t = s + 1
                for b in range(2):
                    i = s * 2 + b
                    if b == 0 and t.within(0, NS):
                        for g in range(4):
                            n = t * 4 + (g + 1)
                            need(pool, qk_mid_ready, n, apart=True)
                            nc.gpsimd.tensor_tensor(parts[:, g % 2, 2], rest[:], parts[:, g % 2, 1],
                                                    ALU.subtract).then_inc(qk_lo_ready, 1)
                            if g == 1 and (i - 1).within(0, NB):
                                inv_std(i, ln2_mv, ln2_eps, ln2_rstd, i, 2, 3)
                    elif (i - 1).within(0, NB):
                        inv_std(i, ln2_mv, ln2_eps, ln2_rstd, i, 2, 3)
                    if (i - 1).within(0, NB):
                        hb = (b + 1) % 2
                        need(pool, x1hat_ready, i, apart=True)
                        nc.gpsimd.tensor_tensor(h2[:, hb], h2[:, hb], cb1_row[:], ALU.mult).then_inc(h2_scaled, 1)
                        need(pool, h2_scaled, i, apart=True)
                        nc.gpsimd.tensor_tensor(h2[:, hb], h2[:, hb], sb_row[:], ALU.add).then_inc(h2_ready, 1)
                    if b == 1 and (s + 2).within(0, NS):
                        ln1(s + 2)

            pool.wait_ge(consts_ready, 1)
            pool.wait_ge(mod_rows_full, 1)
            first = 2 * H * ST
            link(nc.gpsimd.memset(stacks[KROWS:KROWS + 2, first:2 * KT * 6 * D].bitcast(fp32), TWO_ONES))
            for m, at in enumerate((2, 0, 1)):
                pool.wait_ge(wT_full, (m + 1) * KT)
                first = 2 * KT * 6 * D + at * 2 * KT * D
                link(nc.gpsimd.memset(stacks[KROWS:KROWS + 2, first:first + 2 * KT * D].bitcast(fp32), TWO_ONES))
            pool.wait_ge(setup_done, 1)
            link(nc.gpsimd.tensor_scalar(mask_first, mask[:], 1.0, None, ALU.mult))
            for g in range(4):
                rows = mask_first[32 * g:32 * g + 32, :]
                link(nc.gpsimd.affine_select(out=rows, in_=rows, compare_op=ALU.is_ge, fill=LOW, base=32 * g - W,
                                             pattern=[[1, SK]], channel_multiplier=0))
            link(nc.gpsimd.memset(maskT_first[:, 0], LOW))
            nc.gpsimd.tensor_scalar(maskT_first[:, 1], maskT[:, 1], 1.0, None, ALU.mult).then_inc(first_masks_ready, 1)
            ln1(Count(None, 0, 0))
            turns(pool, body)

        @block.scalar
        def _(act):
            act.wait_ge(c_loaded, 16)
            nc.scalar.activation(c_col[:, 1, :], c_col[:, 0, :], ACT.Exp, scale=-1.0).then_inc(silu_exp, 1)
            for m in range(4):
                for k in range(KT):
                    n = m * KT + k
                    act.wait_ge(wT_full, n + 1)
                    if m:
                        act.wait_ge(wT_split, 2 * (n - KT + 1))
                        act.wait_ge(wb_full, m)
                    nc.scalar.activation(wT[:, k, :], ps[:, k, :], ACT.Copy).then_inc(wT_copied, 1)

            def body(s):
                t = s + 1
                for b in range(2):
                    i = s * 2 + b
                    if (i - 1).within(0, NB):
                        need(act, pv_done, i * 8)
                        nc.scalar.activation(heads_sb[:, 1], heads_ps[1], ACT.Copy).then_inc(heads_copied, 1)
                    if b == 0 and t.within(0, NS):
                        for n in range(2):
                            need(act, xT_full, t * 2 + (n + 1))
                            bank = bank_of("xT", 0, n).rearrange("p (k t) -> p k t", k=2)
                            nc.scalar.activation(hT_hi[:, 2 * n:2 * n + 2, :], bank, ACT.Copy).then_inc(hT_hi_ready, 1)
                    if b == 0 and t.within(0, NS):
                        qk_hi(s, 0)
                    if (i - 1).within(0, NB):
                        need(act, attnT_full, i)
                        bank = bank_of("attnT", b, 0).rearrange("p (k t) -> p k t", k=KT)
                        nc.scalar.activation(attnT_hi[:], bank, ACT.Copy).then_inc(attnT_hi_ready, 1)
                    if b == 0 and t.within(0, NS):
                        for g in range(1, 4):
                            qk_hi(s, g)
                    if i.within(0, NB):
                        for u in range(NPAIR):
                            if u in MASKED:
                                need(act, st_masked, masked(i, u))
                            else:
                                need(act, st_full, i * NPAIR + (u + 1))
                            nc.scalar.activation(probs[:, u % RING], st_ps[u % 2], ACT.Exp).then_inc(exp_done, 1)
                            if u == 11:
                                need(act, pv_done, i * 8 + 4)
                                nc.scalar.activation(heads_sb[:, 0], heads_ps[0], ACT.Copy).then_inc(heads_copied, 1)
                    if (i + 1).within(0, NB):
                        need(act, mT_full, i + 2)
                        bank = bank_of("mT", b, 0)
                        nc.scalar.activation(mT[:, 0, :], bank[0:H, 0:W], ACT.Copy, scale=-1.0).then_inc(mT_hi_ready, 1)

            def qk_hi(s, g):
                t = s + 1
                need(act, qk_full, t * 4 + (g + 1))
                need(act, parts_stored[g % 2], t * 96 + 48 * (g // 2))
                bank = bank_of("qk", 0, g).rearrange("p (m t) -> p m t", m=2)
                for m in range(2):
                    mt = 2 * (g % 2) + m
                    nc.scalar.activation(parts[:, g % 2, 0, m], bank[:, m], ACT.Identity,
                                         bias=qk_bias[:, g // 2, mt:mt + 1]).then_inc(qk_hi_ready, 1)

            turns(act, body)

        @block.vector
        def _(dve):
            done = [0]

            def link(ins):
                done[0] += 1
                ins.then_inc(setup_chain, 1)
                dve.wait_ge(setup_chain, done[0])

            dve.wait_ge(silu_exp, 1)
            link(nc.vector.tensor_scalar(c_col[:, 2, :], c_col[:, 1, :], 1.0, None, ALU.add))
            link(nc.vector.reciprocal(c_col[:, 3, :], c_col[:, 2, :]))
            link(nc.vector.tensor_tensor(c_col[:, 2, :], c_col[:, 3, :], c_col[:, 0, :], ALU.mult))
            nc.vector.tensor_copy(silu_bc, c_col[:, 2, :].unsqueeze(2).to_broadcast([128, KT, 128])).then_inc(silu_ready, 1)
            dve.wait_ge(mod_cols_full, 1)
            link(nc.vector.tensor_copy(cols[:].rearrange("p a k -> p (a k)"), misc_ps[0][:, 0:3 * KT]))
            link(nc.vector.tensor_scalar(w_scale[:, 0], cols[:, 1], 1.0, None, ALU.add))
            link(nc.vector.tensor_scalar(w_scale[:, 1], w_scale[:, 0], SCALE, None, ALU.mult))

            def gate(dst, g, t0, t1):
                link(nc.vector.tensor_scalar(t0, g, -1.0, None, ALU.mult))
                link(nc.vector.tensor_tensor(t0, t0, g, ALU.max))
                link(nc.vector.tensor_scalar(t0, t0, 0.25, None, ALU.max))
                link(nc.vector.tensor_scalar(t1, g, 0.0, 2.0, ALU.is_ge, ALU.mult))
                link(nc.vector.tensor_scalar(t1, t1, -1.0, None, ALU.add))
                link(nc.vector.tensor_tensor(dst, t0, t1, ALU.mult))

            gate(cols[:, 2], cols[:, 2], g_tmp[:, 0], g_tmp[:, 1])
            nc.vector.tensor_copy(sa_bc, cols[:, 0, :].unsqueeze(2).to_broadcast([128, KT, 128])).then_inc(mod_ready, 1)
            dve.wait_ge(mod_rows_full, 1)
            link(nc.vector.tensor_scalar(cb1_row[:], ps[:, 4, :], 1.0, None, ALU.add))
            link(nc.vector.tensor_copy(sb_row[:], ps[:, 5, :]))
            link(nc.vector.tensor_copy(gb_row[:], misc_ps[1]))
            gate(gb_row[:], gb_row[:], h2[:, 1, :], attn[:])
            dve.wait_ge(w_loaded["o"], 16)
            for k in range(KT):
                ins = nc.vector.tensor_scalar(w_nat["o"][:, k, :], w_nat["o"][:, k, :], cols[:, 2, k:k + 1], None, ALU.mult)
            ins.then_inc(rows_ready, 1)
            for m, name in enumerate(MATS):
                for k in range(KT):
                    dve.wait_ge(wT_copied, m * KT + k + 1)
                    scale = 1.0 if name == "o" else w_scale[:, int(name == "q"), k:k + 1]
                    nc.vector.tensor_scalar(w_hi[name][:, k, :], wT[:, k, :], scale, None, ALU.mult).then_inc(wT_split, 1)
                    dve.wait_ge(wT_split, 2 * (m * KT + k) + 1)
                    nc.vector.scalar_tensor_tensor(w_lo[name][:, k, :], wT[:, k, :], scale,
                                                   w_hi[name][:, k, :].bitcast(fp32), ALU.mult, ALU.subtract).then_inc(wT_split, 1)
                if name == "v":
                    dve.wait_ge(wb_full, 1)
                    link(nc.vector.tensor_copy(vb_row[:], ps[:, 4, :]))
                if name == "q":
                    dve.wait_ge(wb_full, 2)
                    link(nc.vector.tensor_scalar(qk_bias[:, 0], ps[:, 5, 0:KT], SCALE, None, ALU.mult))
                if name == "k":
                    dve.wait_ge(wb_full, 3)
                    link(nc.vector.tensor_copy(qk_bias[:, 1], misc_ps[1][:, 0:KT]))
            dve.wait_ge(mod_rows_full, 1)
            link(nc.vector.memset(k_stack[0:KROWS, :, 0:W], 0.0))
            link(nc.vector.memset(ps[:, 4, :], 0.0))
            nc.vector.memset(ps[:, 5, :], 0.0).then_inc(setup_done, 1)

            def ln1(t):
                p = t.parity
                need(dve, x_loaded[p], (t - p).half() * 16 + 16)
                for b in range(2):
                    nc.vector.bn_stats(stats[:, b, :], x_in[:, p, b, :]).then_inc(ln1_stats, 1)
                need(dve, ln1_stats, t * 2 + 2, apart=True)
                for b in range(2):
                    nc.vector.bn_aggr(mv[:, b, :], stats[:, b, :]).then_inc(ln1_mv, 1)

            def ln1_apply(t):
                p = t.parity
                need(dve, ln1_rstd, t + 1)
                for b in range(2):
                    nc.vector.tensor_scalar(x_in[:, p, b, :], x_in[:, p, b, :], mv[:, b, 0:1], rstd[:, b:b + 1],
                                            ALU.subtract, ALU.mult).then_inc(xhat_ready, 1)

            def divide(s, b, half, i):
                n = i * 2 + (half + 1)
                need(dve, headsT_full, n)
                bank = bank_of("headsT", b, half).rearrange("p (h e) -> p h e", e=32)
                den = r_den[:, half * 16:(half + 1) * 16]
                nc.vector.reciprocal(den, bank[:, :, DK]).then_inc(den_ready, 1)
                need(dve, den_ready, n)
                nc.vector.tensor_tensor(attn[:, half * 256:(half + 1) * 256].rearrange("p (h e) -> p h e", e=DK),
                                        bank[:, :, 0:DK], den.unsqueeze(2).to_broadcast([128, 16, DK]),
                                        ALU.mult).then_inc(attn_ready, 1)

            def body(s):
                t = s + 1
                for b in range(2):
                    i = s * 2 + b
                    tail = (i - 1).within(0, NB)
                    hb = (b + 1) % 2
                    if b == 0 and t.within(0, NS):
                        for n in range(2):
                            need(dve, hT_hi_ready, t * 2 + (n + 1))
                            bank = bank_of("xT", 0, n).rearrange("p (k t) -> p k t", k=2)
                            nc.vector.tensor_tensor(hT_lo[:, 2 * n:2 * n + 2, :], bank,
                                                    hT_hi[:, 2 * n:2 * n + 2, :].bitcast(fp32), ALU.subtract).then_inc(hT_ready, 1)
                    if b == 1 and t.within(0, NS):
                        values(s, 0)
                    if tail:
                        divide(s, b, 1, i - 1)
                    if b == 0 and t.within(0, NS):
                        qk_rest(s, 0)
                    if tail:
                        need(dve, attnT_hi_ready, i)
                        bank = bank_of("attnT", b, 0).rearrange("p (k t) -> p k t", k=KT)
                        nc.vector.tensor_tensor(attnT_lo[:], bank, attnT_hi[:].bitcast(fp32), ALU.subtract).then_inc(attnT_ready, 1)
                    if b == 0 and t.within(0, NS):
                        qk_rest(s, 1)
                    if b == 1 and t.within(0, NS):
                        values(s, 1)
                    if tail:
                        need(dve, y_full, i)
                        need(dve, x1_loaded[hb], (s if b else s - 1) * 16 + 16)
                        nc.vector.tensor_tensor(x1[:, hb], bank_of("y", b, 0), x1[:, hb], ALU.add).then_inc(x1_ready, 1)
                        need(dve, x1_ready, i)
                        nc.vector.bn_stats(stats[:, 2, :], x1[:, hb]).then_inc(ln2_stats, 1)
                        need(dve, ln2_stats, i, apart=True)
                        nc.vector.bn_aggr(mv[:, 2, :], stats[:, 2, :]).then_inc(ln2_mv, 1)
                    if b == 0 and t.within(0, NS):
                        qk_rest(s, 2)
                        qk_rest(s, 3)
                    if tail and not (i + 1).within(0, NB):
                        normalise(i, hb)
                    for u in range(NPAIR):
                        if i.within(0, NB) and u in MASKED:
                            need(dve, st_full, i * NPAIR + (u + 1))
                            m = maskT_first if i.k is None and i.b == 0 else maskT[:]
                            bank = st_ps[u % 2].rearrange("p (h f) t -> p h (f t)", h=2)
                            nc.vector.tensor_tensor(bank, bank, m.rearrange("p f t -> p (f t)").unsqueeze(1).to_broadcast(
                                [128, 2, 2 * W]), ALU.add).then_inc(st_masked, 1)
                        if (i + 1).within(0, NB) and u < NSG:
                            need(dve, s_full, (i + 1) * NSG + (u + 1))
                            n = min(SG, H - u * SG)
                            nc.vector.tensor_reduce(row_max[:, u * SG:u * SG + n], s_ps[u % 2][:, 0:n, :], AX, ALU.max).then_inc(max_done, 1)
                            if u == 2 and tail:
                                normalise(i, hb)
                            if b == 1 and u == 5 and (s + 2).within(0, NS):
                                ln1(s + 2)
                            if b == 1 and u == 8 and (s + 2).within(0, NS):
                                ln1_apply(s + 2)
                        if tail and u == 11:
                            need(dve, h2_ready, i)
                            nc.vector.tensor_reduce(h2_max[:, bass.ds((i - 1).value(), 1)], h2[:, hb], AX, ALU.max,
                                                    apply_absolute_value=True).then_inc(h2_max_done, 1)
                        if u == 13 and i.within(0, NB):
                            divide(s, b, 0, i)
                    if (i + 1).within(0, NB):
                        need(dve, mT_hi_ready, i + 2)
                        bank = bank_of("mT", b, 0)
                        nc.vector.scalar_tensor_tensor(mT[:, 1, :], bank[0:H, 0:W], -1.0, mT[:, 0, :],
                                                       ALU.mult, ALU.subtract).then_inc(mT_ready, 1)
                if s.k is None and s.b == NS - 1:
                    dve.wait_ge(wf_loaded, 16)
                    nc.vector.tensor_reduce(q8[:, 1:2], wf, AX, ALU.max, apply_absolute_value=True).then_inc(wf_max_ready, 1)

            def normalise(i, hb):
                need(dve, ln2_rstd, i)
                nc.vector.tensor_scalar(h2[:, hb], x1[:, hb], mv[:, 2, 0:1], rstd[:, 2:3],
                                        ALU.subtract, ALU.mult).then_inc(x1hat_ready, 1)

            def values(s, n):
                t = s + 1
                need(dve, v_full, t * 2 + (n + 1))
                slots = [1 + 2 * t.parity + n] + ([0] if t.parity and n else [])
                for at in slots:
                    ins = nc.vector.tensor_tensor(v_tok[:, at, :, 0:DK],
                                                  bank_of("v", 1, n).rearrange("p (h e) -> p h e", e=DK),
                                                  vb_row[:].rearrange("p (h e) -> p h e", e=DK), ALU.add)
                ins.then_inc(v_ready, 1)

            def qk_rest(s, g):
                t = s + 1
                need(dve, qk_hi_ready, t * 8 + (2 * g + 2))
                need(dve, qk_lo_ready, t * 4 + g)
                bank = bank_of("qk", 0, g).rearrange("p (m t) -> p m t", m=2)
                for m in range(2):
                    mt = 2 * (g % 2) + m
                    ins = nc.vector.scalar_tensor_tensor(rest[:, m], bank[:, m], qk_bias[:, g // 2, mt:mt + 1],
                                                         parts[:, g % 2, 0, m], ALU.add, ALU.subtract)
                ins.then_inc(qk_rest_ready, 1)
                need(dve, qk_rest_ready, t * 4 + (g + 1))
                nc.vector.tensor_copy(parts[:, g % 2, 1], rest[:]).then_inc(qk_mid_ready, 1)

            ln1(Count(None, 0, 0))
            ln1_apply(Count(None, 0, 0))
            turns(dve, body)
            dve.wait_ge(wf_max_ready, 1)

        @block.tensor
        def _(pe):
            pe.wait_ge(silu_ready, 1)
            pe.wait_ge(wmod_loaded, 96)
            for a in range(3):
                for k in range(KT):
                    for kk in range(KT):
                        ins = nc.tensor.matmul(misc_ps[0][:, a * KT + k:a * KT + k + 1],
                                               wmod_sb[:, kk, a * D + k * 128:a * D + (k + 1) * 128],
                                               c_col[:, 2, kk:kk + 1], start=(kk == 0), stop=(kk == KT - 1))
            ins.then_inc(mod_cols_full, 1)
            for a, bank in ((3, ps[:, 5, :]), (4, ps[:, 4, :]), (5, misc_ps[1])):
                for kk in range(KT):
                    ins = nc.tensor.matmul(bank, silu_bc[:, kk, :], wmod_sb[:, kk, a * D:(a + 1) * D],
                                           start=(kk == 0), stop=(kk == KT - 1))
            ins.then_inc(mod_rows_full, 1)
            pe.wait_ge(consts_ready, 1)
            pe.wait_ge(rows_ready, 1)
            for m, name in enumerate(MATS):
                pe.wait_ge(w_loaded[name], 16)
                for k in range(KT):
                    if m:
                        pe.wait_ge(wT_copied, (m - 1) * KT + k + 1)
                    for o in range(KT):
                        ins = nc.tensor.transpose(ps[:, k, o * 128:(o + 1) * 128],
                                                  w_nat[name][:, o, k * 128:(k + 1) * 128], ident_f[:])
                    ins.then_inc(wT_full, 1)
                pe.wait_ge(wT_copied, (m + 1) * KT)
                if name == "v":
                    for k in range(KT):
                        ins = nc.tensor.matmul(ps[:, 4, :], sa_bc[:, k, :], wT[:, k, :], start=(k == 0), stop=(k == KT - 1))
                    ins.then_inc(wb_full, 1)
                elif name in "qk":
                    bank = ps[:, 5, :] if name == "q" else misc_ps[1]
                    for o in range(KT):
                        for k in range(KT):
                            ins = nc.tensor.matmul(bank[:, o:o + 1], wT[:, k, o * 128:(o + 1) * 128],
                                                   cols[:, 0, k:k + 1], start=(k == 0), stop=(k == KT - 1))
                    ins.then_inc(wb_full, 1)
            pe.wait_ge(setup_done, 1)
            pe.wait_ge(wT_split, 2 * 4 * KT)
            pe.wait_ge(first_masks_ready, 1)

            def heads_to_tokens(s, b, half, i):
                bank = take_bank(pe, s, "headsT", b, half)
                need(pe, heads_copied, i * 2 + (half + 1))
                for g in range(4):
                    ins = nc.tensor.transpose(bank[:, g * 128:(g + 1) * 128], heads_sb[:, half, g, :], ident_f[:])
                ins.then_inc(headsT_full, 1)

            def x_to_features(s, n):
                t = s + 1
                bank = take_bank(pe, s, "xT", 0, n).rearrange("p (k t) -> p k t", k=2)
                need(pe, xhat_ready, t * 2 + 2)
                for k in range(2):
                    for b in range(2):
                        kk = 2 * n + k
                        ins = nc.tensor.transpose(bank[:, k, b * W:(b + 1) * W],
                                                  x_in[:, t.parity, b, kk * 128:(kk + 1) * 128], ident_f[:])
                ins.then_inc(xT_full, 1)

            def project_qk(s, g):
                t = s + 1
                name = "q" if g < 2 else "k"
                bank = take_bank(pe, s, "qk", 0, g).rearrange("p (m t) -> p m t", m=2)
                for m in range(2):
                    o = (2 * (g % 2) + m) * 128
                    pairs = [(w, h, k) for k in range(KT) for w, h in ((w_hi, hT_hi), (w_hi, hT_lo), (w_lo, hT_hi))]
                    for n, (w, h, k) in enumerate(pairs):
                        if g == 0 and m == 0 and n % 6 == 0:
                            need(pe, hT_ready, t * 2 + (n // 6 + 1))
                        ins = nc.tensor.matmul(bank[:, m], w[name][:, k, o:o + 128], h[:, k, :],
                                               start=(n == 0), stop=(n == len(pairs) - 1))
                ins.then_inc(qk_full, 1)

            def project_v(s, n, first, last):
                bank = take_bank(pe, s, "v", 1, n) if first == 0 else bank_of("v", 1, n)
                pairs = [(w, h, k) for k in range(KT) for h, w in ((hT_hi, w_hi), (hT_hi, w_lo), (hT_lo, w_hi))]
                for m, (w, h, k) in enumerate(pairs):
                    if first <= k < last:
                        ins = nc.tensor.matmul(bank, h[:, k, n * W:(n + 1) * W], w["v"][:, k, :],
                                               start=(m == 0), stop=(m == len(pairs) - 1))
                if last == KT:
                    ins.then_inc(v_full, 1)

            def attn_to_features(s, b, i):
                bank = take_bank(pe, s, "attnT", b, 0).rearrange("p (k t) -> p k t", k=KT)
                need(pe, attn_ready, i * 2 + 2)
                for k in range(KT):
                    ins = nc.tensor.transpose(bank[:, k], attn[:, k * 128:(k + 1) * 128], ident_f[:])
                ins.then_inc(attnT_full, 1)

            def project_out(s, b, i):
                bank = take_bank(pe, s, "y", b, 0)
                need(pe, attnT_ready, i + 1)
                pairs = [(w, h, k) for k in range(KT) for h, w in ((attnT_hi, w_hi), (attnT_hi, w_lo), (attnT_lo, w_hi))]
                for m, (w, h, k) in enumerate(pairs):
                    ins = nc.tensor.matmul(bank, h[:, k, :], w["o"][:, k, :], start=(m == 0), stop=(m == len(pairs) - 1))
                ins.then_inc(y_full, 1)

            def scores(s, b, u, j):
                jb = (b + 1) % 2
                js = s if b == 0 else s + 1
                first = j.k is None and j.b == 0
                if u == 0:
                    need(pe, q_loaded, js * 96 + 96)
                    need(pe, k_loaded[jb], js * 96 + 96)
                    if jb == 0 and js.parity == 0:
                        need(pe, k_carry_loaded, js.half() * 96)
                if u < 2:
                    take_bank(pe, s, "scores", b, u)
                else:
                    need(pe, max_done, j * NSG + (u - 1))
                n = min(SG, H - u * SG)
                bank = s_ps[u % 2]
                for edge in [slice(0, SK)] if first else [slice(0, 32), slice(W, SK)]:
                    edge_mask = mask_first[:, edge] if first else mask[:, edge]
                    nc.tensor.matmul(bank[:, 0:n, edge], ident_b[:],
                                     edge_mask.unsqueeze(1).to_broadcast([128, n, edge.stop - edge.start]),
                                     start=(edge.start == 0), stop=False, skip_group_check=True)
                for h in range(n):
                    for g in range(4):
                        at = k_at(js, jb) + 32 * g
                        ins = nc.tensor.matmul(bank[32 * g:32 * g + 32, h, :],
                                               q_stack[0:KROWS, js.parity, u * SG + h, jb * W + 32 * g:jb * W + 32 * g + 32],
                                               k_stack[0:KROWS, u * SG + h, at:at + SK],
                                               start=False, stop=True, skip_group_check=True)
                ins.then_inc(s_full, 1)

            def scores_transposed(s, b, u, i):
                if u == 0:
                    need(pe, m_loaded, i * 32 + 32)
                need(pe, exp_done, i * NPAIR + (u - 1))
                m = maskT_first if i.k is None and i.b == 0 else maskT[:]
                if u not in MASKED:
                    nc.tensor.matmul(st_ps[u % 2].rearrange("p (h f) t -> p h (f t)", h=2), ident_b[:],
                                     m.rearrange("p f t -> p (f t)").unsqueeze(1).to_broadcast([128, 2, 2 * W]),
                                     start=True, stop=False, skip_group_check=True)
                for h in range(2):
                    for f in range(2):
                        at = k_at(s, b) + f * W
                        ins = nc.tensor.matmul(st_ps[u % 2][:, 2 * h + f],
                                               k_stack[0:KROWS + 2, 2 * u + h, at:at + W],
                                               q_stack[0:KROWS + 2, s.parity, 2 * u + h, b * W:(b + 1) * W],
                                               start=(u in MASKED and h == 0 and f == 0), stop=True, skip_group_check=True)
                ins.then_inc(st_full, 1)

            def weigh_values(s, b, g, i):
                if g == 0:
                    need(pe, v_ready, i + 1)
                if g % 4 == 0:
                    need(pe, heads_copied, i * 2 + (g // 4 - 1))
                need(pe, exp_done, i * NPAIR + (2 * g + 2))
                for f in range(2):
                    for q in range(4):
                        h = 4 * g + q
                        ins = nc.tensor.matmul(heads_ps[g // 4][32 * q:32 * q + HR, g % 4, :],
                                               v_tok[:, 2 * s.parity + b + f, h, :],
                                               probs[:, (h // 2) % RING, 2 * (h % 2) + f, :],
                                               start=(f == 0), stop=(f == 1), skip_group_check=True)
                ins.then_inc(pv_done, 1)

            def body(s):
                t = s + 1
                for b in range(2):
                    i = s * 2 + b
                    tail, attend, score = (i - 1).within(0, NB), i.within(0, NB), (i + 1).within(0, NB)
                    proj = t.within(0, NS)
                    if proj and b == 0:
                        x_to_features(s, 0)
                        x_to_features(s, 1)
                    if proj and b == 1:
                        project_v(s, 0, 0, KT)
                    if tail:
                        heads_to_tokens(s, b, 1, i - 1)
                    if proj and b == 0:
                        project_qk(s, 0)
                    if proj and b == 1:
                        project_v(s, 1, 0, KT // 2)
                    if tail:
                        attn_to_features(s, b, i - 1)
                    if proj and b == 0:
                        project_qk(s, 1)
                    if proj and b == 1:
                        project_v(s, 1, KT // 2, KT)
                    if tail:
                        project_out(s, b, i - 1)
                    if proj and b == 0:
                        project_qk(s, 2)
                        project_qk(s, 3)
                    for u in range(NPAIR):
                        if attend:
                            scores_transposed(s, b, u, i)
                        if score and u < NSG:
                            scores(s, b, u, i + 1)
                        if attend and u % 2 and u >= 3:
                            weigh_values(s, b, (u - 3) // 2, i)
                        if attend and u == 13:
                            heads_to_tokens(s, b, 0, i)
                    if score:
                        bank = take_bank(pe, s, "mT", b, 0)
                        need(pe, max_done, (i + 2) * NSG)
                        nc.tensor.transpose(bank[0:H, 0:W], row_max[:], ident_f[:]).then_inc(mT_full, 1)
                    if attend:
                        weigh_values(s, b, 7, i)

            turns(pe, body)

        first_phase.close()
        block = ctx.enter_context(nc.Block())
        taken = [2 * 2 * KT * D]

        def carve(elems, dt, pattern=None, **sizes):
            size = elems * (2 if dt == fp32 or dt == u32 else 1)
            piece = stacks[:, taken[0]:taken[0] + size]
            taken[0] += size
            piece = piece if dt == bf16 else piece.bitcast(dt)
            return piece.rearrange(pattern, **sizes) if pattern else piece

        wf_unit = carve(KT * D, fp32)
        wf_magic = carve(KT * D, fp32)
        wf_q = carve(KT * D, bf16, "p (k d) -> p k d", k=KT)
        wf_qT = carve(KT * D, bf16, "p (k d) -> p k d", k=KT)
        bias_part = carve(3 * D, bf16, "p (a d) -> p a d", a=3)
        bias_rows = carve(D, bf16)
        ones_rows = carve(128, bf16)
        ratio = carve(16, fp32)
        magic = carve(4 * D, fp32, "p (r d) -> p r d", r=4)
        hq = carve(4 * D, bf16, "p (r d) -> p r d", r=4)
        hqT = carve(4 * KT * W, bf16, "p (r k t) -> p r k t", r=4, k=KT)
        result = carve(4 * D, fp32, "p (r d) -> p r d", r=4)

        amax_own = sem("amax_own")
        amax_ready = sem("amax_ready")
        prep = sem("prep")
        scales_ready = sem("scales_ready")
        wf_ready = sem("wf_ready")
        wfT_full = sem("wfT_full")
        wfT_ready = sem("wfT_ready")
        bias_ready = sem("bias_ready")
        unit_ready = sem("unit_ready")
        power_ready = sem("power_ready")
        magic_ready = sem("magic_ready")
        rounded_ready = sem("rounded_ready")
        hq_ready = sem("hq_ready")
        hqT_full = sem("hqT_full")
        hqT_ready = sem("hqT_ready")
        z_full = sem("z_full")
        z_scaled = sem("z_scaled")
        result_ready = [sem("result_ready_even"), sem("result_ready_odd")]
        result_stored = [sem(f"result_stored_{r}") for r in range(4)]

        EXPONENT, SMALLEST, MAGIC = 0x7F800000, 2.0 ** -6, 1.5 * 2.0 ** 20

        def rounds(eng, body):
            for n in range(8):
                body(Count(None, 0, n))
            with eng.Fori(0, (NB - 12) // 4) as k:
                for n in range(8, 12):
                    body(Count(k, 4, n))
            for n in range(NB - 4, NB + 5):
                body(Count(None, 0, n))

        def fills(n):
            return (n - n.slot).over(4)

        hqT_ps = [ps[:, r, 0:KT * W // 2].bitcast(bf16).rearrange("p (k t) -> p k t", k=KT) for r in range(4)]
        z_ps = [ps[:, 4 + r, :] for r in range(4)]
        wfT_ps = [ps[:, 4 + k, 0:D // 2].bitcast(bf16) for k in range(KT)]

        def finish(ops, eng, n):
            need(eng, z_scaled, n + 1)
            need(eng, x1_back[n.slot], fills(n) * 16 + 16)
            ops.tensor_tensor(result[:, n.slot], result[:, n.slot], x1_in[:, n.slot], ALU.add).then_inc(result_ready[n.parity], 1)

        def results(n):
            return (n - n.parity).half() + 1

        @block.sync
        def _(sp):
            def load_h2(n):
                need(sp, hq_ready, n - 3, apart=True)
                sp.dma_start(h2_in[:, n.slot], h2_dram[bass.ds(n.value(), 1)].rearrange("a p d -> p (a d)")
                             ).then_inc(h2_loaded[n.slot], 16)

            def load_x1(n):
                if not (n.k is None and n.b < 4):
                    need(sp, result_ready[n.parity], results(n - 4), apart=True)
                sp.dma_start(x1_in[:, n.slot], x1_dram[bass.ds(n.value(), 1)].rearrange("a p d -> p (a d)")
                             ).then_inc(x1_back[n.slot], 16)

            def store(n):
                need(sp, result_ready[n.parity], results(n), apart=True)
                sp.dma_start(ob[bass.ds(n.value(), 1)].rearrange("a p d -> p (a d)"), result[:, n.slot]
                             ).then_inc(result_stored[n.slot], 16)

            def body(n):
                if (n + 2).within(4, NB):
                    load_h2(n + 2)
                if (n - 5).within(0, NB):
                    store(n - 5)
                if (n - 1).within(0, NB):
                    load_x1(n - 1)

            rounds(sp, body)
            for r in range(4):
                sp.wait_ge(result_stored[r], 16 * (NB // 4))

        @block.gpsimd
        def _(pool):
            pool.wait_ge(amax_own, 1)
            nc.gpsimd.partition_all_reduce(q8[:, 2:4], q8[:, 0:2], 128, bass.bass_isa.ReduceOp.max).then_inc(amax_ready, 1)

            def round_up(n):
                need(pool, magic_ready, n + 1)
                nc.gpsimd.tensor_tensor(h2_in[:, n.slot], h2_in[:, n.slot], magic[:, n.slot], ALU.add).then_inc(rounded_ready, 1)

            def body(n):
                if n.within(0, NB):
                    round_up(n)
                if (n - 3).within(0, NB) and n.parity:
                    finish(nc.gpsimd, pool, n - 3)

            rounds(pool, body)

        @block.scalar
        def _(act):
            act.wait_ge(scales_ready, 1)

            def units(n):
                need(act, h2_loaded[n.slot], fills(n) * 16 + 16)
                nc.scalar.activation(h2_in[:, n.slot], h2_in[:, n.slot], ACT.Copy, scale=q8[:, 6:7]).then_inc(unit_ready, 1)

            def turn_over(n):
                need(act, hqT_full, n + 1)
                nc.scalar.activation(hqT[:, n.slot], hqT_ps[n.slot], ACT.Copy).then_inc(hqT_ready, 1)

            def body(n):
                if n.within(0, NB):
                    units(n)
                if n.k is None and n.b == 2:
                    for k in range(KT):
                        act.wait_ge(wfT_full, k + 1)
                        nc.scalar.activation(wf_qT[:, k], wfT_ps[k], ACT.Copy).then_inc(wfT_ready, 1)
                if (n - 2).within(0, NB):
                    turn_over(n - 2)

            rounds(act, body)

        @block.vector
        def _(dve):
            done = [0]

            def link(ins):
                done[0] += 1
                ins.then_inc(prep, 1)
                dve.wait_ge(prep, done[0])

            nc.vector.tensor_reduce(q8[:, 0:1], h2_max[:], AX, ALU.max).then_inc(amax_own, 1)
            dve.wait_ge(amax_ready, 1)
            link(nc.vector.tensor_tensor(q8[:, 3:4], q8[:, 3:4], q8[:, 2:3], ALU.max))
            link(nc.vector.tensor_scalar(q8[:, 4:6], q8[:, 2:4], 1.0 / QMAX, None, ALU.mult))
            link(nc.vector.reciprocal(q8[:, 6:8], q8[:, 4:6]))
            link(nc.vector.tensor_tensor(ratio[:, 0:1], q8[:, 4:5], q8[:, 5:6], ALU.mult))
            nc.vector.tensor_tensor(ratio[:, 1:2], q8[:, 6:7], q8[:, 7:8], ALU.mult).then_inc(scales_ready, 1)
            dve.wait_ge(scales_ready, 1)

            def powers(n):
                p = n.slot
                need(dve, unit_ready, n + 1)
                nc.vector.tensor_scalar(magic[:, p].bitcast(u32), h2_in[:, p].bitcast(u32), EXPONENT, None, ALU.bitwise_and).then_inc(power_ready, 1)
                need(dve, power_ready, n + 1)
                nc.vector.tensor_scalar(magic[:, p], magic[:, p], SMALLEST, MAGIC, ALU.max, ALU.mult).then_inc(magic_ready, 1)

            def grid(n):
                p = n.slot
                need(dve, rounded_ready, n + 1)
                need(dve, hqT_full, n - 3)
                nc.vector.tensor_tensor(hq[:, p], h2_in[:, p], magic[:, p], ALU.subtract).then_inc(hq_ready, 1)

            def scaled(n):
                p = n.slot
                need(dve, z_full, n + 1)
                need(dve, result_stored[p], fills(n) * 16)
                nc.vector.tensor_tensor(result[:, p], z_ps[p], gb_row[:], ALU.mult).then_inc(z_scaled, 1)

            def weight():
                link(nc.vector.tensor_scalar(wf_unit, wf, q8[:, 7:8], None, ALU.mult))
                link(nc.vector.tensor_scalar(wf_magic.bitcast(u32), wf_unit.bitcast(u32), EXPONENT, None, ALU.bitwise_and))
                link(nc.vector.tensor_scalar(wf_magic, wf_magic, SMALLEST, MAGIC, ALU.max, ALU.mult))
                link(nc.vector.tensor_tensor(wf_unit, wf_unit, wf_magic, ALU.add))
                nc.vector.tensor_tensor(wf_q.rearrange("p k d -> p (k d)"), wf_unit, wf_magic, ALU.subtract).then_inc(wf_ready, 1)

            def rows():
                link(nc.vector.tensor_scalar(gb_row[:], gb_row[:], ratio[:, 0:1], None, ALU.mult))
                link(nc.vector.tensor_scalar(bias_all, bias_all, ratio[:, 1:2], None, ALU.mult))
                for a in range(3):
                    link(nc.vector.tensor_copy(bias_part[:, a], bias_all))
                    if a < 2:
                        link(nc.vector.tensor_tensor(bias_all, bias_all, bias_part[:, a], ALU.subtract))
                link(nc.vector.memset(bias_rows, 0.0))
                link(nc.vector.memset(ones_rows, 1.0))
                for a in range(3):
                    ins = nc.vector.tensor_copy(bias_rows[32 * a:32 * a + 1], bias_part[32 * a:32 * a + 1, a])
                ins.then_inc(bias_ready, 1)

            def body(n):
                if n.within(0, NB):
                    powers(n)
                if n.k is None and n.b == 0:
                    weight()
                if (n - 1).within(0, NB):
                    grid(n - 1)
                if n.k is None and n.b == 1:
                    rows()
                if (n - 3).within(0, NB):
                    scaled(n - 3)
                if (n - 4).within(0, NB) and n.parity:
                    finish(nc.vector, dve, n - 4)

            rounds(dve, body)

        @block.tensor
        def _(pe):
            pe.wait_ge(wf_ready, 1)
            for k in range(KT):
                for o in range(KT):
                    ins = nc.tensor.transpose(wfT_ps[k][:, o * 128:(o + 1) * 128], wf_q[:, o, k * 128:(k + 1) * 128], ident_b[:])
                ins.then_inc(wfT_full, 1)

            def transposed(n):
                need(pe, hq_ready, n + 1)
                need(pe, hqT_ready, n - 3)
                for k in range(KT):
                    ins = nc.tensor.transpose(hqT_ps[n.slot][:, k], hq[:, n.slot, k * 128:(k + 1) * 128], ident_b[:])
                ins.then_inc(hqT_full, 1)

            def product(n):
                need(pe, hqT_ready, n + 1)
                need(pe, z_scaled, n - 3)
                for k in range(KT):
                    nc.tensor.matmul(z_ps[n.slot], hqT[:, n.slot, k], wf_qT[:, k], start=(k == 0), stop=False)
                nc.tensor.matmul(z_ps[n.slot], ones_rows[0:96], bias_rows[0:96], start=False, stop=True).then_inc(z_full, 1)

            def body(n):
                if n.within(0, NB):
                    transposed(n)
                if n.k is None and n.b == 1:
                    pe.wait_ge(wfT_ready, KT)
                    pe.wait_ge(bias_ready, 1)
                if (n - 1).within(0, NB):
                    product(n - 1)

            rounds(pe, body)


_INS = ['L0_attn_x', 'L0_attn_Wq', 'L0_attn_Wk', 'L0_attn_Wv', 'L0_attn_Wo', 'L0_ffn_weight', 'L0_ffn_bias', 'L0_c', 'L0_wmod']
_OUTS = [((1, 4096, 512), 'float32')]


def kernel(**inputs):
    import numpy as _np
    import concourse.bacc as _bacc
    from concourse import mybir as _mybir
    from concourse.bass_utils import run_bass_kernel_spmd as _run

    nc = _bacc.Bacc("TRN2", target_bir_lowering=False, num_devices=1)
    arrays, args = {}, []
    for name in _INS:
        a = _np.ascontiguousarray(inputs[name])
        arrays[f"in_{name}_dram"] = a
        args.append(nc.dram_tensor(f"in_{name}_dram", a.shape, _mybir.dt.from_np(a.dtype), kind="ExternalInput").ap())
    for i, (shape, dtype) in enumerate(_OUTS):
        dt = _mybir.dt.from_np(_np.dtype(dtype))
        args.append(nc.dram_tensor(f"out_{i}_dram", shape, dt, kind="ExternalOutput").ap())
    adaln_block(nc, *args)
    r = _run(nc, [arrays], core_ids=[0])
    return r.results[0]["out_0_dram"]
```

```python
import numpy as np

import concourse.bass as bass
from concourse import mybir
from contextlib import ExitStack


class Count:

    def __init__(self, k, a, b):
        self.k, self.a, self.b = k, (a if k is not None else 0), b

    def __mul__(self, m):
        return Count(self.k, self.a * m, self.b * m)

    def __add__(self, n):
        return Count(self.k, self.a, self.b + n)

    def __sub__(self, n):
        return self + (-n)

    def half(self):
        return Count(self.k, self.a // 2, self.b // 2)

    def over(self, m):
        return Count(self.k, self.a // m, self.b // m)

    @property
    def parity(self):
        return self.b % 2

    @property
    def slot(self):
        return self.b % 4

    def within(self, lo, hi):
        return True if self.k is not None else lo <= self.b < hi

    def value(self):
        return self.b if self.k is None or self.a == 0 else self.k * self.a + self.b


def need(eng, sem, count, apart=False):
    if isinstance(count, Count):
        if count.k is None and count.b <= 0:
            return
        assert count.b > 0, "a looped turn waits for something"
        eng.wait_ge(sem, count.value())
        if apart and count.k is not None:
            eng.nop(nofuse=True)
    elif count > 0:
        eng.wait_ge(sem, count)


def adaln_block(nc: bass.Bass, x, Wq, Wk, Wv, Wo, Wf, bias, c, wmod, out):
    fp32 = mybir.dt.float32
    fp32r = mybir.dt.float32r
    bf16 = mybir.dt.bfloat16
    u32 = mybir.dt.uint32
    ALU = mybir.AluOpType
    ACT = mybir.ActivationFunctionType
    AX = mybir.AxisListType.X

    T, D = x.shape[1], x.shape[2]
    H, DK = 32, D // 32
    W = 128
    KT = D // 128
    NB = T // W
    ST = 2 * W
    NS = T // ST
    SK = W + 32
    SG = 3
    NSG = (H + SG - 1) // SG
    NPAIR = H // 2
    RING = 4
    HR = DK + 1
    KROWS = 6 * DK
    EPS = 1e-5
    SCALE = 1.0 / DK ** 0.5
    QMAX = 448.0 * 0.8
    LOW = -3.0e38
    TWO_ONES = float(np.array([0x3F803F80], np.uint32).view(np.float32)[0])

    xs = x.rearrange("a (s b p) d -> (a s) p b d", b=2, p=128)
    xb = x.rearrange("a (n p) d -> (a n) p d", p=128)
    ob = out.rearrange("a (n p) d -> (a n) p d", p=128)

    ctx = ExitStack()
    with ctx:
        def sb(name, shape, dt):
            return ctx.enter_context(nc.sbuf_tensor(name, shape, dt))

        def sem(name):
            return ctx.enter_context(nc.semaphore(name))

        q_parts_dram = nc.dram_tensor("q_parts", [3, D, T], bf16, kind="Internal").ap()
        k_parts_dram = nc.dram_tensor("k_parts", [3, D, T], bf16, kind="Internal").ap()
        x1_dram = nc.dram_tensor("x1_scratch", [NB, 128, D], fp32, kind="Internal").ap()
        h2_dram = nc.dram_tensor("h2_scratch", [NB, 128, D], fp32, kind="Internal").ap()
        parts_dram = {"q": q_parts_dram, "k": k_parts_dram}

        w_hi = {n: sb(f"w{n}_hi", [128, KT, D], fp32r) for n in "qkvo"}
        w_lo = {n: sb(f"w{n}_lo", [128, KT, D], fp32r) for n in "qkvo"}
        Q_SLOTS, K_SLOTS = (0, 0, 0, 1, 1, 2), (0, 1, 2, 0, 1, 0)
        stacks = sb("stacks", [128, H * (2 * ST + W + 2 * ST)], bf16)
        q_stack = stacks[:, 0:2 * H * ST].rearrange("p (r h t) -> p r h t", r=2, h=H)
        k_stack = stacks[:, 2 * H * ST:].rearrange("p (h t) -> p h t", h=H)

        x_in = sb("x_in", [128, 2, 2, D], fp32)
        hT_hi = sb("hT_hi", [128, KT, ST], fp32r)
        hT_lo = sb("hT_lo", [128, KT, ST], fp32r)
        parts = sb("parts", [128, 2, 3, 2, ST], bf16)
        rest = sb("rest", [128, 2, ST], fp32)
        v_tok = sb("v_tok", [128, 5, H, HR], fp32)
        probs = sb("probs", [128, RING, 4, W], fp32)
        cb1_row = sb("cb1_row", [128, D], fp32)
        sb_row = sb("sb_row", [128, D], fp32)
        gb_row = sb("gb_row", [128, D], fp32)
        vb_row = sb("vb_row", [128, D], fp32)
        work = sb("work", [128, 2 * D + 2 * D], fp32)
        x1 = work[:, 0:2 * D].rearrange("p (r d) -> p r d", r=2)
        heads_sb = work[:, 2 * D:4 * D].rearrange("p (f g t) -> p f g t", f=2, g=4)
        h2 = sb("h2", [128, 2, D], fp32)
        attn = sb("attn", [128, D], fp32)
        attnT_hi = sb("attnT_hi", [128, KT, W], fp32r)
        attnT_lo = sb("attnT_lo", [128, KT, W], fp32r)
        ident_f = sb("ident_f", [128, 128], fp32)
        ident_b = sb("ident_b", [128, 128], bf16)
        mask = sb("mask", [128, SK], bf16)
        maskT = sb("maskT", [128, 2, W], bf16)
        first_masks = h2[:, 0, :].bitcast(bf16)
        mask_first = first_masks[:, 0:SK]
        maskT_first = first_masks[:, 2 * W:4 * W].rearrange("p (f t) -> p f t", f=2)
        row_max = sb("row_max", [128, H], fp32)
        r_den = sb("r_den", [128, H], fp32)
        mT = sb("mT", [H, 2, W], bf16)
        stats = sb("stats", [128, 3, 6], fp32)
        mv = sb("mv", [128, 3, 2], fp32)
        rstd = sb("rstd", [128, 3], fp32)
        m_half = sb("m_half", [128, 3], fp32)
        h2_max = sb("h2_max", [128, NB], fp32)
        cols = sb("cols", [128, 3, KT], fp32)
        c_col = sb("c_col", [128, 4, KT], fp32)
        g_tmp = sb("g_tmp", [128, 2, KT], fp32)
        w_scale = sb("w_scale", [128, 2, KT], fp32)
        qk_bias = sb("qk_bias", [128, 2, KT], fp32)
        q8 = sb("q8", [128, 8], fp32)

        ps = ctx.enter_context(nc.psum_tensor("ps", [128, 8, 512], fp32))
        st_ps = [ps[:, 0 + b, :].rearrange("p (f t) -> p f t", f=4) for b in range(2)]
        s_ps = [ps[:, 2 + b, 0:SG * SK].rearrange("p (h t) -> p h t", h=SG) for b in range(2)]
        heads_ps = [ps[:, 4 + b, :].rearrange("p (g t) -> p g t", g=4) for b in range(2)]

        c_loaded = sem("c_loaded")
        wmod_loaded = [sem(f"wmod_loaded_{a}") for a in range(6)]
        w_loaded = {n: sem(f"w{n}_loaded") for n in "qkvo"}
        consts_step = sem("consts_step")
        consts_ready = sem("consts_ready")
        first_masks_ready = sem("first_masks_ready")
        ident_ready = sem("ident_ready")
        silu_exp = sem("silu_exp")
        setup_chain = sem("setup_chain")
        silu_ready = sem("silu_ready")
        mod_rows_full = sem("mod_rows_full")
        mod_rows_copied = sem("mod_rows_copied")
        mod_cols_full = sem("mod_cols_full")
        mod_ready = sem("mod_ready")
        wo_gated = sem("wo_gated")
        wT_full = sem("wT_full")
        wT_copied = sem("wT_copied")
        w_hi_ready = sem("w_hi_ready")
        w_lo_ready = sem("w_lo_ready")
        wb_full = sem("wb_full")
        wb_copied = sem("wb_copied")
        wb_cols_full = sem("wb_cols_full")
        wb_read = sem("wb_read")
        sb_copied = sem("sb_copied")
        heads_zeroed = sem("heads_zeroed")
        x_loaded = [sem("x_loaded_even"), sem("x_loaded_odd")]
        x1_loaded = [sem("xres_loaded_0"), sem("xres_loaded_1")]
        ln1_stats = sem("ln1_stats")
        ln1_mv = sem("ln1_mv")
        ln1_eps = sem("ln1_eps")
        ln1_rstd = sem("ln1_rstd")
        xhat_ready = sem("xhat_ready")
        xT_full = sem("xT_full")
        hT_hi_ready = sem("hT_hi_ready")
        hT_ready = sem("hT_ready")
        qk_full = sem("qk_full")
        qk_hi_ready = sem("qk_hi_ready")
        qk_rest_ready = sem("qk_rest_ready")
        qk_mid_ready = sem("qk_mid_ready")
        qk_lo_ready = sem("qk_lo_ready")
        parts_stored = [sem("parts_stored_0"), sem("parts_stored_1")]
        q_loaded = sem("q_loaded")
        k_loaded = [sem("k_loaded_0"), sem("k_loaded_1")]
        k_carry_loaded = sem("k_carry_loaded")
        v_full = sem("v_full")
        v_ready = sem("v_ready")
        s_full = sem("s_full")
        max_done = sem("max_done")
        mT_full = sem("mT_full")
        mT_hi_ready = sem("mT_hi_ready")
        mT_ready = sem("mT_ready")
        m_loaded = sem("m_loaded")
        st_full = sem("st_full")
        st_masked = sem("st_masked")
        exp_done = sem("exp_done")
        pv_done = sem("pv_done")
        heads_copied = sem("heads_copied")
        headsT_full = sem("headsT_full")
        den_ready = sem("den_ready")
        attn_ready = sem("attn_ready")
        attnT_full = sem("attnT_full")
        attnT_hi_ready = sem("attnT_hi_ready")
        attnT_ready = sem("attnT_ready")
        y_full = sem("y_full")
        x1_ready = sem("x1_ready")
        ln2_stats = sem("ln2_stats")
        ln2_mv = sem("ln2_mv")
        ln2_eps = sem("ln2_eps")
        ln2_rstd = sem("ln2_rstd")
        x1hat_ready = sem("x1hat_ready")
        h2_scaled = sem("h2_scaled")
        h2_ready = sem("h2_ready")
        h2_max_done = sem("h2_max_done")
        x1_stored = [sem("x1_stored_0"), sem("x1_stored_1")]
        h2_stored = [sem("h2_stored_0"), sem("h2_stored_1")]

        USES = {("xT", 0, 0): 2, ("xT", 0, 1): 3, ("qk", 0, 0): 7, ("headsT", 0, 1): 6, ("qk", 0, 1): 2,
                ("attnT", 0, 0): 6, ("qk", 0, 2): 3, ("y", 0, 0): 6, ("qk", 0, 3): 7, ("scores", 0, 0): 2,
                ("scores", 0, 1): 3, ("headsT", 0, 0): 6, ("mT", 0, 0): 7,
                ("v", 1, 0): 2, ("headsT", 1, 1): 6, ("v", 1, 1): 3, ("attnT", 1, 0): 7, ("y", 1, 0): 6,
                ("scores", 1, 0): 2, ("scores", 1, 1): 3, ("headsT", 1, 0): 7, ("mT", 1, 0): 6}
        FREED = {"xT": hT_ready, "qk": qk_rest_ready, "v": v_ready, "headsT": attn_ready,
                 "attnT": attnT_ready, "y": x1_ready, "scores": max_done, "mT": mT_ready}

        def nth(s, use):
            kind, b, n = use
            if kind in ("xT", "v"):
                return s * 2 + (2 + n), 2 * NS
            if kind == "qk":
                return s * 4 + (4 + n), 4 * NS
            if kind == "headsT":
                return s * 4 + (2 * b + n if n == 0 else 2 * b - 1), 2 * NB
            if kind in ("attnT", "y"):
                return s * 2 + (b - 1), NB
            if kind == "scores":
                return s * (2 * NSG) + ((b + 1) * NSG + NSG - 1 - (NSG - 1 - n) % 2), NB * NSG
            return s * 2 + (b + 1), NB

        def bank_of(kind, b, n):
            return ps[:, USES[kind, b, n], :]

        def take_bank(pe, s, *use):
            order = [u for u in USES if USES[u] == USES[use]]
            pos, back = order.index(use), s
            while True:
                pos -= 1
                if pos < 0:
                    pos, back = pos + len(order), back - 1
                if back.k is None and back.b < -1:
                    break
                n, total = nth(back, order[pos])
                if n.within(0, total):
                    need(pe, FREED[order[pos][0]], n + 1)
                    break
            return bank_of(*use)

        MASKED = (4, 6, 8, 10, 12)

        def masked(i, u):
            return i * len(MASKED) + (MASKED.index(u) + 1)

        def turns(eng, body):
            body(Count(None, 0, -1))
            body(Count(None, 0, 0))
            with eng.Fori(0, (NS - 4) // 2) as k:
                body(Count(k, 2, 1))
                body(Count(k, 2, 2))
            for s in range(NS - 3, NS + 1):
                body(Count(None, 0, s))

        def k_at(s, b):
            return ST * s.parity + W * b

        late = stacks[:, 0:2 * 2 * KT * D].bitcast(fp32)
        wf = late[:, 0:KT * D]
        x1_in = late[:, KT * D:2 * KT * D].rearrange("p (r d) -> p r d", r=4)
        h2_in = x_in[:].rearrange("p r b d -> p (r b) d")
        bias_all = rest[:].rearrange("p m t -> p (m t)")
        wf_loaded = sem("wf_loaded")
        bias_loaded = sem("bias_loaded")
        h2_loaded = [sem(f"h2_loaded_{r}") for r in range(4)]
        x1_back = [sem(f"x1_back_{r}") for r in range(4)]
        wf_max_ready = sem("wf_max_ready")

        first_phase = ExitStack()
        block = first_phase.enter_context(nc.Block())
        MAT = 2 * KT * D
        WMOD_AT = (5, 4, 0, 1, 2, 3)
        wmod_sb = [stacks[:, at * MAT:(at + 1) * MAT].bitcast(fp32).rearrange("p (k d) -> p k d", k=KT)
                   for at in WMOD_AT]
        w_nat = {"k": stacks[:, 6 * MAT:7 * MAT].bitcast(fp32).rearrange("p (k d) -> p k d", k=KT),
                 "q": work[:].rearrange("p (k d) -> p k d", k=KT),
                 "v": v_tok[:].rearrange("p a h e -> p (a h e)")[:, 0:KT * D].rearrange("p (k d) -> p k d", k=KT),
                 "o": probs[:].rearrange("p r f t -> p (r f t)").rearrange("p (k d) -> p k d", k=KT)}
        silu_bc = attn[:].rearrange("p (k m) -> p k m", k=KT)
        sa_bc = rest[:].rearrange("p m t -> p (m t)").rearrange("p (k m) -> p k m", k=KT)
        first_rows = [cb1_row, sb_row, gb_row]
        MATS = ("k", "q", "v", "o")

        @block.sync
        def _(sp):
            with nc.allow_non_contiguous_dma(reason="512 values, once"):
                sp.dma_start(c_col[:, 0, :], c.rearrange("a (k p) -> p (a k)", p=128)).then_inc(c_loaded, 16)
            def load_x(t):
                sp.dma_start(x_in[:, t.parity],
                             xs[bass.ds(t.value(), 1)].rearrange("a p b d -> p (a b) d")).then_inc(x_loaded[t.parity], 16)

            def load_w(name, w):
                sp.dma_start(w_nat[name], w.rearrange("(k p) d -> p k d", p=128)).then_inc(w_loaded[name], 16)

            def load_wmod(a):
                sp.dma_start(wmod_sb[a], wmod[:, a * D:(a + 1) * D].rearrange("(k p) d -> p k d", p=128)
                             ).then_inc(wmod_loaded[a], 16)

            load_x(Count(None, 0, 0))
            for name, w in (("k", Wk), ("q", Wq), ("v", Wv)):
                load_w(name, w)
            for a in range(3):
                load_wmod(a)
            load_w("o", Wo)
            for a in range(3, 6):
                load_wmod(a)
            load_x(Count(None, 0, 1))
            sp.wait_ge(mod_rows_full, 4)
            sp.wait_ge(w_lo_ready, 4 * KT)

            def store_parts(s, g):
                t = s + 1
                need(sp, qk_lo_ready, t * 4 + (g + 1), apart=True)
                dram = parts_dram["q" if g < 2 else "k"]
                for part in range(3):
                    rows = dram[part, (g % 2) * 2 * 128:((g % 2) * 2 + 2) * 128, :].rearrange("(m p) t -> p m t", p=128)
                    sp.dma_start(rows[:, :, bass.ds((t * ST).value(), ST)],
                                 parts[:, g % 2, part]).then_inc(parts_stored[g % 2], 16)

            def load_stack(dst, name, slots, start, n, done):
                for row, part in enumerate(slots):
                    src = parts_dram[name][part].rearrange("(h d) t -> d h t", d=DK)
                    sp.dma_start(dst[row * DK:(row + 1) * DK], src[:, :, bass.ds(start, n)]).then_inc(done, 16)

            def load_second():
                sp.wait_ge(st_full, (NS - 1) * 2 * NPAIR)
                sp.wait_ge(xT_full, 2 * NS)
                sp.wait_ge(qk_lo_ready, 4 * NS)
                sp.dma_start(wf.rearrange("p (k d) -> p k d", k=KT), Wf.rearrange("(k p) d -> p k d", p=128)).then_inc(wf_loaded, 16)
                sp.dma_start(bias_all, bias.unsqueeze(0).to_broadcast([128, D])).then_inc(bias_loaded, 16)
                for n in range(4):
                    sp.dma_start(h2_in[:, n], h2_dram[n]).then_inc(h2_loaded[n], 16)

            def body(s):
                t = s + 1
                for b in range(2):
                    i = s * 2 + b
                    if i.within(0, NB):
                        need(sp, h2_stored[b], s * 16, apart=True)
                        need(sp, x1_stored[b], s * 16, apart=True)
                        sp.dma_start(x1[:, b, :], xb[bass.ds(i.value(), 1)].rearrange("a p d -> p (a d)")
                                     ).then_inc(x1_loaded[b], 16)
                    if b == 0 and t.within(0, NS):
                        store_parts(s, 0)
                        store_parts(s, 1)
                        need(sp, parts_stored[0], t * 96 + 48, apart=True)
                        need(sp, parts_stored[1], t * 96 + 48, apart=True)
                        need(sp, st_full, s * (2 * NPAIR), apart=True)
                        load_stack(q_stack[:, t.parity], "q", Q_SLOTS, (t * ST).value(), ST, q_loaded)
                        store_parts(s, 2)
                        store_parts(s, 3)
                        need(sp, parts_stored[0], t * 96 + 96, apart=True)
                        need(sp, parts_stored[1], t * 96 + 96, apart=True)
                        load_stack(k_stack[:, :, k_at(t, 0) + W:k_at(t, 0) + 2 * W], "k", K_SLOTS,
                                   (t * ST).value(), W, k_loaded[0])
                    if b == 0 and (s + 3).within(2, NS):
                        need(sp, xT_full, t * 2 + 2, apart=True)
                        load_x(s + 3)
                    j = i + 1
                    if (i - 1).within(0, NB):
                        store_block(i - 1, (b + 1) % 2, s if b else s - 1)
                    if j.within(0, NB):
                        need(sp, mT_ready, j + 1, apart=True)
                        jb = (b + 1) % 2
                        jp = s.parity if b == 0 else t.parity
                        for part in range(2):
                            sp.dma_start(q_stack[KROWS + part:KROWS + part + 1, jp, :, jb * W:(jb + 1) * W],
                                         mT[:, part, :]).then_inc(m_loaded, 16)
                    if b == 0 and t.within(0, NS):
                        need(sp, st_full, (s * 2 + 1) * NPAIR, apart=True)
                        load_stack(k_stack[:, :, k_at(t, 1) + W:k_at(t, 1) + 2 * W], "k", K_SLOTS,
                                   (t * ST + W).value(), W, k_loaded[1])
                        if t.parity:
                            load_stack(k_stack[:, :, 0:W], "k", K_SLOTS, (t * ST + W).value(), W, k_carry_loaded)

                    if b == 0 and s.k is None and s.b == NS - 1:
                        load_second()

            def store_block(i, b, s):
                need(sp, ln2_mv, i + 1, apart=True)
                need(sp, x1hat_ready, i + 1, apart=True)
                sp.dma_start(x1_dram[bass.ds(i.value(), 1)].rearrange("a p d -> p (a d)"), x1[:, b, :]).then_inc(x1_stored[b], 16)
                need(sp, h2_ready, i + 1, apart=True)
                sp.dma_start(h2_dram[bass.ds(i.value(), 1)].rearrange("a p d -> p (a d)"), h2[:, b, :]).then_inc(h2_stored[b], 16)

            turns(sp, body)
            for b in range(2):
                sp.wait_ge(x1_stored[b], 16 * (NB // 2))
                sp.wait_ge(h2_stored[b], 16 * (NB // 2))

        @block.gpsimd
        def _(pool):
            done = [0]

            def link(ins):
                done[0] += 1
                ins.then_inc(consts_step, 1)
                pool.wait_ge(consts_step, done[0])

            link(nc.gpsimd.memset(ident_f[:], 1.0))
            link(nc.gpsimd.affine_select(out=ident_f[:], in_=ident_f[:], compare_op=ALU.is_equal, fill=0.0, base=0,
                                         pattern=[[-1, 128]], channel_multiplier=1))
            nc.gpsimd.tensor_scalar(ident_b[:], ident_f[:], 1.0, None, ALU.mult).then_inc(ident_ready, 1)
            pool.wait_ge(ident_ready, 1)
            link(nc.gpsimd.memset(m_half[:], -0.5))
            link(nc.gpsimd.memset(mask[:], 0.0))
            for g in range(4):
                rows = mask[32 * g:32 * g + 32, :]
                link(nc.gpsimd.affine_select(out=rows, in_=rows, compare_op=ALU.is_ge, fill=LOW, base=0,
                                             pattern=[[1, SK]], channel_multiplier=-1))
                link(nc.gpsimd.affine_select(out=rows, in_=rows, compare_op=ALU.is_ge, fill=LOW, base=W,
                                             pattern=[[-1, SK]], channel_multiplier=1))
            link(nc.gpsimd.memset(maskT[:], 0.0))
            link(nc.gpsimd.affine_select(out=maskT[:, 0], in_=maskT[:, 0], compare_op=ALU.is_ge, fill=LOW, base=0,
                                         pattern=[[-1, W]], channel_multiplier=1))
            link(nc.gpsimd.affine_select(out=maskT[:, 1], in_=maskT[:, 1], compare_op=ALU.is_ge, fill=LOW, base=0,
                                         pattern=[[1, W]], channel_multiplier=-1))

            def inv_std(at, mv_ready, eps_added, ready, n, first, last):
                need(pool, mv_ready, n, apart=True)
                nc.gpsimd.tensor_scalar(rstd[:, first:last], mv[:, first:last, 1], EPS, None, ALU.add).then_inc(eps_added, 1)
                need(pool, eps_added, at, apart=True)
                nc.gpsimd.tensor_tensor(rstd[:, first:last], rstd[:, first:last], m_half[:, first:last],
                                        ALU.pow).then_inc(ready, 1)

            def ln1(t):
                inv_std(t + 1, ln1_mv, ln1_eps, ln1_rstd, t * 2 + 2, 0, 2)

            def body(s):
                t = s + 1
                for b in range(2):
                    i = s * 2 + b
                    if b == 0 and t.within(0, NS):
                        for g in range(4):
                            n = t * 4 + (g + 1)
                            need(pool, qk_mid_ready, n, apart=True)
                            nc.gpsimd.tensor_tensor(parts[:, g % 2, 2], rest[:], parts[:, g % 2, 1],
                                                    ALU.subtract).then_inc(qk_lo_ready, 1)
                            if g == 2 and (i - 1).within(0, NB):
                                inv_std(i, ln2_mv, ln2_eps, ln2_rstd, i, 2, 3)
                    elif (i - 1).within(0, NB):
                        inv_std(i, ln2_mv, ln2_eps, ln2_rstd, i, 2, 3)
                    if (i - 1).within(0, NB):
                        hb = (b + 1) % 2
                        need(pool, x1hat_ready, i, apart=True)
                        nc.gpsimd.tensor_tensor(h2[:, hb], h2[:, hb], cb1_row[:], ALU.mult).then_inc(h2_scaled, 1)
                        need(pool, h2_scaled, i, apart=True)
                        nc.gpsimd.tensor_tensor(h2[:, hb], h2[:, hb], sb_row[:], ALU.add).then_inc(h2_ready, 1)
                    if b == 1 and (s + 2).within(0, NS):
                        ln1(s + 2)

            link(nc.gpsimd.tensor_scalar(mask_first, mask[:], 1.0, None, ALU.mult))
            for g in range(4):
                rows = mask_first[32 * g:32 * g + 32, :]
                link(nc.gpsimd.affine_select(out=rows, in_=rows, compare_op=ALU.is_ge, fill=LOW, base=32 * g - W,
                                             pattern=[[1, SK]], channel_multiplier=0))
            link(nc.gpsimd.memset(maskT_first[:, 0], LOW))
            nc.gpsimd.tensor_scalar(maskT_first[:, 1], maskT[:, 1], 1.0, None, ALU.mult).then_inc(first_masks_ready, 1)
            pool.wait_ge(first_masks_ready, 1)
            ln1(Count(None, 0, 0))
            pool.wait_ge(ln1_rstd, 1)

            def ones(first, last):
                link(nc.gpsimd.memset(stacks[KROWS:KROWS + 2, first:last].bitcast(fp32), TWO_ONES))

            ones(7 * MAT, 9 * MAT)
            pool.wait_ge(mod_rows_full, 2)
            ones(4 * MAT, 6 * MAT)
            pool.wait_ge(wb_full, 1)
            pool.wait_ge(w_lo_ready, KT)
            ones(6 * MAT, 7 * MAT)
            link(nc.gpsimd.memset(k_stack[0:KROWS, :, 0:W].bitcast(fp32), 0.0))
            pool.wait_ge(wb_full, 3)
            pool.wait_ge(w_lo_ready, 3 * KT)
            nc.gpsimd.memset(v_tok[:], 1.0).then_inc(consts_ready, 1)
            pool.wait_ge(consts_ready, 1)
            turns(pool, body)

        @block.scalar
        def _(act):
            act.wait_ge(c_loaded, 16)
            nc.scalar.activation(c_col[:, 1, :], c_col[:, 0, :], ACT.Exp, scale=-1.0).then_inc(silu_exp, 1)
            for m, name in enumerate(MATS[:3]):
                act.wait_ge(wT_full, m + 1)
                for k in range(KT):
                    nc.scalar.activation(w_nat[name][:, k, :], ps[:, 4 * (m % 2) + k, :], ACT.Copy).then_inc(wT_copied, 1)
            for a in range(3):
                act.wait_ge(mod_rows_full, a + 1)
                nc.scalar.activation(first_rows[a][0:1, :], ps[0:1, 4 + a, :], ACT.Copy).then_inc(mod_rows_copied, 1)
            act.wait_ge(mod_ready, 1)
            for name in MATS[:3]:
                for k in range(KT):
                    nc.scalar.activation(w_hi[name][:, k, :], w_nat[name][:, k, :], ACT.Copy,
                                         scale=w_scale[:, int(name == "q"), k:k + 1]).then_inc(w_hi_ready, 1)
            for m in range(2):
                act.wait_ge(wb_full, m + 1)
                nc.scalar.activation(first_rows[m][0:1, :], ps[0:1, m, :], ACT.Copy).then_inc(wb_copied, 1)
            act.wait_ge(mod_rows_full, 4)
            act.wait_ge(wb_cols_full, 1)
            nc.scalar.activation(sb_row[:], ps[:, 4, :], ACT.Copy).then_inc(sb_copied, 1)
            act.wait_ge(wT_full, 4)
            for k in range(KT):
                nc.scalar.activation(w_hi["o"][:, k, :], ps[:, k, :], ACT.Copy).then_inc(w_hi_ready, 1)

            def body(s):
                t = s + 1
                for b in range(2):
                    i = s * 2 + b
                    if b == 0 and t.within(0, NS):
                        for n in range(2):
                            need(act, xT_full, t * 2 + (n + 1))
                            bank = bank_of("xT", 0, n).rearrange("p (k t) -> p k t", k=2)
                            nc.scalar.activation(hT_hi[:, 2 * n:2 * n + 2, :], bank, ACT.Copy).then_inc(hT_hi_ready, 1)
                    if (i - 1).within(0, NB):
                        need(act, pv_done, i * 8)
                        nc.scalar.activation(heads_sb[:, 1], heads_ps[1], ACT.Copy).then_inc(heads_copied, 1)
                    if b == 0 and t.within(0, NS):
                        qk_hi(s, 0)
                        qk_hi(s, 1)
                    if (i - 1).within(0, NB):
                        need(act, attnT_full, i)
                        bank = bank_of("attnT", b, 0).rearrange("p (k t) -> p k t", k=KT)
                        nc.scalar.activation(attnT_hi[:], bank, ACT.Copy).then_inc(attnT_hi_ready, 1)
                    if b == 0 and t.within(0, NS):
                        qk_hi(s, 2)
                        qk_hi(s, 3)
                    if i.within(0, NB):
                        for u in range(NPAIR):
                            if u in MASKED:
                                need(act, st_masked, masked(i, u))
                            else:
                                need(act, st_full, i * NPAIR + (u + 1))
                            nc.scalar.activation(probs[:, u % RING], st_ps[u % 2], ACT.Exp).then_inc(exp_done, 1)
                            if u == 11:
                                need(act, pv_done, i * 8 + 4)
                                nc.scalar.activation(heads_sb[:, 0], heads_ps[0], ACT.Copy).then_inc(heads_copied, 1)
                    if (i + 1).within(0, NB):
                        need(act, mT_full, i + 2)
                        bank = bank_of("mT", b, 0)
                        nc.scalar.activation(mT[:, 0, :], bank[0:H, 0:W], ACT.Copy, scale=-1.0).then_inc(mT_hi_ready, 1)

            def qk_hi(s, g):
                t = s + 1
                need(act, qk_full, t * 4 + (g + 1))
                need(act, parts_stored[g % 2], t * 96 + 48 * (g // 2))
                bank = bank_of("qk", 0, g).rearrange("p (m t) -> p m t", m=2)
                for m in range(2):
                    mt = 2 * (g % 2) + m
                    nc.scalar.activation(parts[:, g % 2, 0, m], bank[:, m], ACT.Identity,
                                         bias=qk_bias[:, g // 2, mt:mt + 1]).then_inc(qk_hi_ready, 1)

            turns(act, body)

        @block.vector
        def _(dve):
            done = [0]

            def link(ins):
                done[0] += 1
                ins.then_inc(setup_chain, 1)
                dve.wait_ge(setup_chain, done[0])

            dve.wait_ge(silu_exp, 1)
            link(nc.vector.tensor_scalar(c_col[:, 2, :], c_col[:, 1, :], 1.0, None, ALU.add))
            link(nc.vector.reciprocal(c_col[:, 3, :], c_col[:, 2, :]))
            link(nc.vector.tensor_tensor(c_col[:, 2, :], c_col[:, 3, :], c_col[:, 0, :], ALU.mult))
            nc.vector.tensor_copy(silu_bc, c_col[:, 2, :].unsqueeze(2).to_broadcast([128, KT, 128])).then_inc(silu_ready, 1)
            def ln1_stats_of(t, b):
                p = t.parity
                need(dve, x_loaded[p], (t - p).half() * 16 + 16)
                nc.vector.bn_stats(stats[:, b, :], x_in[:, p, b, :]).then_inc(ln1_stats, 1)

            def ln1_aggregate(t):
                need(dve, ln1_stats, t * 2 + 2, apart=True)
                for b in range(2):
                    nc.vector.bn_aggr(mv[:, b, :], stats[:, b, :]).then_inc(ln1_mv, 1)

            def ln1_apply(t, b):
                p = t.parity
                need(dve, ln1_rstd, t + 1)
                nc.vector.tensor_scalar(x_in[:, p, b, :], x_in[:, p, b, :], mv[:, b, 0:1], rstd[:, b:b + 1],
                                        ALU.subtract, ALU.mult).then_inc(xhat_ready, 1)

            for b in range(2):
                ln1_stats_of(Count(None, 0, 0), b)
            ln1_aggregate(Count(None, 0, 0))
            for b in range(2):
                ln1_apply(Count(None, 0, 0), b)
            dve.wait_ge(mod_cols_full, 1)
            link(nc.vector.tensor_copy(cols[:].rearrange("p a k -> p (a k)"), ps[:, 7, 0:3 * KT]))
            link(nc.vector.tensor_scalar(w_scale[:, 0], cols[:, 1], 1.0, None, ALU.add))
            link(nc.vector.tensor_scalar(w_scale[:, 1], w_scale[:, 0], SCALE, None, ALU.mult))
            nc.vector.tensor_copy(sa_bc, cols[:, 0, :].unsqueeze(2).to_broadcast([128, KT, 128])).then_inc(mod_ready, 1)

            def gate(dst, g, t0, t1):
                link(nc.vector.tensor_scalar(t0, g, -1.0, None, ALU.mult))
                link(nc.vector.tensor_tensor(t0, t0, g, ALU.max))
                link(nc.vector.tensor_scalar(t0, t0, 0.25, None, ALU.max))
                link(nc.vector.tensor_scalar(t1, g, 0.0, 2.0, ALU.is_ge, ALU.mult))
                link(nc.vector.tensor_scalar(t1, t1, -1.0, None, ALU.add))
                link(nc.vector.tensor_tensor(dst, t0, t1, ALU.mult))

            gate(cols[:, 2], cols[:, 2], g_tmp[:, 0], g_tmp[:, 1])
            dve.wait_ge(w_loaded["o"], 16)
            for k in range(KT):
                nc.vector.tensor_scalar(w_nat["o"][:, k, :], w_nat["o"][:, k, :], cols[:, 2, k:k + 1], None,
                                        ALU.mult).then_inc(wo_gated, 1)

            def low_parts(m, name):
                for k in range(KT):
                    dve.wait_ge(w_hi_ready, m * KT + k + 1)
                    hi = w_hi[name][:, k, :].bitcast(fp32)
                    if name == "o":
                        ins = nc.vector.tensor_tensor(w_lo[name][:, k, :], ps[:, k, :], hi, ALU.subtract)
                    else:
                        ins = nc.vector.scalar_tensor_tensor(w_lo[name][:, k, :], w_nat[name][:, k, :],
                                                             w_scale[:, int(name == "q"), k:k + 1], hi, ALU.mult, ALU.subtract)
                    ins.then_inc(w_lo_ready, 1)

            for m, name in enumerate(MATS[:3]):
                low_parts(m, name)
            dve.wait_ge(wb_full, 3)
            nc.vector.tensor_copy(vb_row[:], ps[:, 2, :]).then_inc(wb_read, 1)
            dve.wait_ge(wb_cols_full, 1)
            nc.vector.tensor_copy(qk_bias[:, 1], ps[:, 3, 0:KT]).then_inc(wb_read, 1)
            nc.vector.tensor_scalar(qk_bias[:, 0], ps[:, 3, KT:2 * KT], SCALE, None, ALU.mult).then_inc(wb_read, 1)
            low_parts(3, "o")

            def last_rows():
                dve.wait_ge(mod_rows_full, 6)
                dve.wait_ge(sb_copied, 1)
                link(nc.vector.tensor_scalar(cb1_row[:], ps[:, 5, :], 1.0, None, ALU.add))
                link(nc.vector.tensor_copy(gb_row[:], ps[:, 4, :]))
                link(nc.vector.memset(ps[:, 4, :], 0.0))
                nc.vector.memset(ps[:, 5, :], 0.0).then_inc(heads_zeroed, 1)
                gate(gb_row[:], gb_row[:], h2[:, 1, :], attn[:])

            def divide(s, b, half, i):
                n = i * 2 + (half + 1)
                need(dve, headsT_full, n)
                bank = bank_of("headsT", b, half).rearrange("p (h e) -> p h e", e=32)
                den = r_den[:, half * 16:(half + 1) * 16]
                nc.vector.reciprocal(den, bank[:, :, DK]).then_inc(den_ready, 1)
                need(dve, den_ready, n)
                nc.vector.tensor_tensor(attn[:, half * 256:(half + 1) * 256].rearrange("p (h e) -> p h e", e=DK),
                                        bank[:, :, 0:DK], den.unsqueeze(2).to_broadcast([128, 16, DK]),
                                        ALU.mult).then_inc(attn_ready, 1)

            def body(s):
                t = s + 1
                for b in range(2):
                    i = s * 2 + b
                    tail = (i - 1).within(0, NB)
                    hb = (b + 1) % 2
                    if b == 0 and t.within(0, NS):
                        for n in range(2):
                            need(dve, hT_hi_ready, t * 2 + (n + 1))
                            bank = bank_of("xT", 0, n).rearrange("p (k t) -> p k t", k=2)
                            nc.vector.tensor_tensor(hT_lo[:, 2 * n:2 * n + 2, :], bank,
                                                    hT_hi[:, 2 * n:2 * n + 2, :].bitcast(fp32), ALU.subtract).then_inc(hT_ready, 1)
                    if b == 0 and t.within(0, NS):
                        qk_rest(s, 0)
                    if b == 1 and t.within(0, NS):
                        values(s, 0)
                    if tail:
                        divide(s, b, 1, i - 1)
                    if b == 0 and t.within(0, NS):
                        qk_rest(s, 1)
                    if tail:
                        need(dve, attnT_hi_ready, i)
                        bank = bank_of("attnT", b, 0).rearrange("p (k t) -> p k t", k=KT)
                        nc.vector.tensor_tensor(attnT_lo[:], bank, attnT_hi[:].bitcast(fp32), ALU.subtract).then_inc(attnT_ready, 1)
                    if b == 0 and t.within(0, NS):
                        qk_rest(s, 2)
                    if b == 1 and t.within(0, NS):
                        values(s, 1)
                        if s.k is None and s.b == -1:
                            last_rows()
                    if tail:
                        need(dve, y_full, i)
                        need(dve, x1_loaded[hb], (s if b else s - 1) * 16 + 16)
                        nc.vector.tensor_tensor(x1[:, hb], bank_of("y", b, 0), x1[:, hb], ALU.add).then_inc(x1_ready, 1)
                        need(dve, x1_ready, i)
                        nc.vector.bn_stats(stats[:, 2, :], x1[:, hb]).then_inc(ln2_stats, 1)
                        need(dve, ln2_stats, i, apart=True)
                        nc.vector.bn_aggr(mv[:, 2, :], stats[:, 2, :]).then_inc(ln2_mv, 1)
                    if b == 0 and t.within(0, NS) and not (i + 1).within(0, NB):
                        qk_rest(s, 3)
                    if tail and not (i + 1).within(0, NB):
                        normalise(i, hb)
                    for u in range(NPAIR):
                        if i.within(0, NB) and u in MASKED:
                            need(dve, st_full, i * NPAIR + (u + 1))
                            m = maskT_first if i.k is None and i.b == 0 else maskT[:]
                            bank = st_ps[u % 2].rearrange("p (h f) t -> p h (f t)", h=2)
                            nc.vector.tensor_tensor(bank, bank, m.rearrange("p f t -> p (f t)").unsqueeze(1).to_broadcast(
                                [128, 2, 2 * W]), ALU.add).then_inc(st_masked, 1)
                        if (i + 1).within(0, NB) and u < NSG:
                            need(dve, s_full, (i + 1) * NSG + (u + 1))
                            n = min(SG, H - u * SG)
                            nc.vector.tensor_reduce(row_max[:, u * SG:u * SG + n], s_ps[u % 2][:, 0:n, :], AX, ALU.max).then_inc(max_done, 1)
                            if u == 1 and b == 0 and t.within(0, NS):
                                qk_rest(s, 3)
                            if u == 2 and tail:
                                normalise(i, hb)
                        if b == 1 and (s + 2).within(0, NS):
                            if u in (5, 7):
                                ln1_stats_of(s + 2, (u - 5) // 2)
                            if u == 8:
                                ln1_aggregate(s + 2)
                            if u in (12, 13):
                                ln1_apply(s + 2, u - 12)
                        if u == 13 and i.within(0, NB):
                            divide(s, b, 0, i)
                        if tail and u == 14:
                            need(dve, h2_ready, i)
                            nc.vector.tensor_reduce(h2_max[:, bass.ds((i - 1).value(), 1)], h2[:, hb], AX, ALU.max,
                                                    apply_absolute_value=True).then_inc(h2_max_done, 1)
                    if (i + 1).within(0, NB):
                        need(dve, mT_hi_ready, i + 2)
                        bank = bank_of("mT", b, 0)
                        nc.vector.scalar_tensor_tensor(mT[:, 1, :], bank[0:H, 0:W], -1.0, mT[:, 0, :],
                                                       ALU.mult, ALU.subtract).then_inc(mT_ready, 1)
                if s.k is None and s.b == NS - 1:
                    dve.wait_ge(wf_loaded, 16)
                    nc.vector.tensor_reduce(q8[:, 1:2], wf, AX, ALU.max, apply_absolute_value=True).then_inc(wf_max_ready, 1)

            def normalise(i, hb):
                need(dve, ln2_rstd, i)
                nc.vector.tensor_scalar(h2[:, hb], x1[:, hb], mv[:, 2, 0:1], rstd[:, 2:3],
                                        ALU.subtract, ALU.mult).then_inc(x1hat_ready, 1)

            def values(s, n):
                t = s + 1
                if s.k is None and s.b == -1 and n == 0:
                    dve.wait_ge(consts_ready, 1)
                need(dve, v_full, t * 2 + (n + 1))
                slots = [1 + 2 * t.parity + n] + ([0] if t.parity and n else [])
                for at in slots:
                    ins = nc.vector.tensor_tensor(v_tok[:, at, :, 0:DK],
                                                  bank_of("v", 1, n).rearrange("p (h e) -> p h e", e=DK),
                                                  vb_row[:].rearrange("p (h e) -> p h e", e=DK), ALU.add)
                ins.then_inc(v_ready, 1)

            def qk_rest(s, g):
                t = s + 1
                need(dve, qk_hi_ready, t * 8 + (2 * g + 2))
                need(dve, qk_lo_ready, t * 4 + g)
                bank = bank_of("qk", 0, g).rearrange("p (m t) -> p m t", m=2)
                for m in range(2):
                    mt = 2 * (g % 2) + m
                    ins = nc.vector.scalar_tensor_tensor(rest[:, m], bank[:, m], qk_bias[:, g // 2, mt:mt + 1],
                                                         parts[:, g % 2, 0, m], ALU.add, ALU.subtract)
                ins.then_inc(qk_rest_ready, 1)
                need(dve, qk_rest_ready, t * 4 + (g + 1))
                nc.vector.tensor_copy(parts[:, g % 2, 1], rest[:]).then_inc(qk_mid_ready, 1)

            turns(dve, body)
            dve.wait_ge(wf_max_ready, 1)

        @block.tensor
        def _(pe):
            def transpose_w(name, first_bank):
                for k in range(KT):
                    for o in range(KT):
                        ins = nc.tensor.transpose(ps[:, first_bank + k, o * 128:(o + 1) * 128],
                                                  w_nat[name][:, o, k * 128:(k + 1) * 128], ident_f[:])
                ins.then_inc(wT_full, 1)

            MOD_BANK = (4, 5, 6, 4, 5, 4)

            def mod_row(a):
                pe.wait_ge(wmod_loaded[a], 16)
                for kk in range(KT):
                    ins = nc.tensor.matmul(ps[:, MOD_BANK[a], :], silu_bc[:, kk, :], wmod_sb[a][:, kk, :],
                                           start=(kk == 0), stop=(kk == KT - 1))
                ins.then_inc(mod_rows_full, 1)

            pe.wait_ge(ident_ready, 1)
            for m, name in enumerate(MATS[:3]):
                pe.wait_ge(w_loaded[name], 16)
                if m == 2:
                    pe.wait_ge(wT_copied, KT)
                transpose_w(name, 4 * (m % 2))
            pe.wait_ge(silu_ready, 1)
            pe.wait_ge(wT_copied, 2 * KT)
            for a in range(3):
                mod_row(a)
            for a in range(3):
                pe.wait_ge(mod_rows_copied, a + 1)
                for k in range(KT):
                    ins = nc.tensor.transpose(ps[:, 7, a * KT + k:a * KT + k + 1],
                                              first_rows[a][0:1, k * 128:(k + 1) * 128], ident_f[0:1, 0:1])
            ins.then_inc(mod_cols_full, 1)
            pe.wait_ge(mod_ready, 1)
            pe.wait_ge(wT_copied, 3 * KT)
            for m, name in enumerate(MATS[:3]):
                for k in range(KT):
                    ins = nc.tensor.matmul(ps[:, m, :], sa_bc[:, k, :], w_nat[name][:, k, :], start=(k == 0), stop=(k == KT - 1))
                ins.then_inc(wb_full, 1)
            mod_row(3)
            for m in range(2):
                pe.wait_ge(wb_copied, m + 1)
                for k in range(KT):
                    ins = nc.tensor.transpose(ps[:, 3, m * KT + k:m * KT + k + 1],
                                              first_rows[m][0:1, k * 128:(k + 1) * 128], ident_f[0:1, 0:1])
            ins.then_inc(wb_cols_full, 1)
            pe.wait_ge(wo_gated, KT)
            pe.wait_ge(wb_read, 3)
            transpose_w("o", 0)
            pe.wait_ge(w_lo_ready, 4 * KT)

            def last_rows():
                mod_row(4)
                pe.wait_ge(sb_copied, 1)
                mod_row(5)
                pe.wait_ge(first_masks_ready, 1)
                pe.wait_ge(consts_ready, 1)

            def heads_to_tokens(s, b, half, i):
                bank = take_bank(pe, s, "headsT", b, half)
                need(pe, heads_copied, i * 2 + (half + 1))
                for g in range(4):
                    ins = nc.tensor.transpose(bank[:, g * 128:(g + 1) * 128], heads_sb[:, half, g, :], ident_f[:])
                ins.then_inc(headsT_full, 1)

            def x_to_features(s, n):
                t = s + 1
                bank = take_bank(pe, s, "xT", 0, n).rearrange("p (k t) -> p k t", k=2)
                need(pe, xhat_ready, t * 2 + 2)
                for k in range(2):
                    for b in range(2):
                        kk = 2 * n + k
                        ins = nc.tensor.transpose(bank[:, k, b * W:(b + 1) * W],
                                                  x_in[:, t.parity, b, kk * 128:(kk + 1) * 128], ident_f[:])
                ins.then_inc(xT_full, 1)

            def project_qk(s, g):
                t = s + 1
                name = "q" if g < 2 else "k"
                bank = take_bank(pe, s, "qk", 0, g).rearrange("p (m t) -> p m t", m=2)
                for m in range(2):
                    o = (2 * (g % 2) + m) * 128
                    pairs = [(w, h, k) for k in range(KT) for w, h in ((w_hi, hT_hi), (w_hi, hT_lo), (w_lo, hT_hi))]
                    for n, (w, h, k) in enumerate(pairs):
                        if g == 0 and m == 0 and n % 6 == 0:
                            need(pe, hT_ready, t * 2 + (n // 6 + 1))
                        ins = nc.tensor.matmul(bank[:, m], w[name][:, k, o:o + 128], h[:, k, :],
                                               start=(n == 0), stop=(n == len(pairs) - 1))
                ins.then_inc(qk_full, 1)

            def project_v(s, n, first, last):
                bank = take_bank(pe, s, "v", 1, n) if first == 0 else bank_of("v", 1, n)
                pairs = [(w, h, k) for k in range(KT) for h, w in ((hT_hi, w_hi), (hT_hi, w_lo), (hT_lo, w_hi))]
                for m, (w, h, k) in enumerate(pairs):
                    if first <= k < last:
                        ins = nc.tensor.matmul(bank, h[:, k, n * W:(n + 1) * W], w["v"][:, k, :],
                                               start=(m == 0), stop=(m == len(pairs) - 1))
                if last == KT:
                    ins.then_inc(v_full, 1)

            def attn_to_features(s, b, i):
                bank = take_bank(pe, s, "attnT", b, 0).rearrange("p (k t) -> p k t", k=KT)
                need(pe, attn_ready, i * 2 + 2)
                for k in range(KT):
                    ins = nc.tensor.transpose(bank[:, k], attn[:, k * 128:(k + 1) * 128], ident_f[:])
                ins.then_inc(attnT_full, 1)

            def project_out(s, b, i):
                bank = take_bank(pe, s, "y", b, 0)
                need(pe, attnT_ready, i + 1)
                pairs = [(w, h, k) for k in range(KT) for h, w in ((attnT_hi, w_hi), (attnT_hi, w_lo), (attnT_lo, w_hi))]
                for m, (w, h, k) in enumerate(pairs):
                    ins = nc.tensor.matmul(bank, h[:, k, :], w["o"][:, k, :], start=(m == 0), stop=(m == len(pairs) - 1))
                ins.then_inc(y_full, 1)

            def scores(s, b, u, j):
                jb = (b + 1) % 2
                js = s if b == 0 else s + 1
                first = j.k is None and j.b == 0
                if u == 0:
                    need(pe, q_loaded, js * 96 + 96)
                    need(pe, k_loaded[jb], js * 96 + 96)
                    if jb == 0 and js.parity == 0:
                        need(pe, k_carry_loaded, js.half() * 96)
                if u < 2:
                    take_bank(pe, s, "scores", b, u)
                else:
                    need(pe, max_done, j * NSG + (u - 1))
                n = min(SG, H - u * SG)
                bank = s_ps[u % 2]
                for edge in [slice(0, SK)] if first else [slice(0, 32), slice(W, SK)]:
                    edge_mask = mask_first[:, edge] if first else mask[:, edge]
                    nc.tensor.matmul(bank[:, 0:n, edge], ident_b[:],
                                     edge_mask.unsqueeze(1).to_broadcast([128, n, edge.stop - edge.start]),
                                     start=(edge.start == 0), stop=False, skip_group_check=True)
                for h in range(n):
                    for g in range(4):
                        at = k_at(js, jb) + 32 * g
                        ins = nc.tensor.matmul(bank[32 * g:32 * g + 32, h, :],
                                               q_stack[0:KROWS, js.parity, u * SG + h, jb * W + 32 * g:jb * W + 32 * g + 32],
                                               k_stack[0:KROWS, u * SG + h, at:at + SK],
                                               start=False, stop=True, skip_group_check=True)
                ins.then_inc(s_full, 1)

            def scores_transposed(s, b, u, i):
                if u == 0:
                    need(pe, m_loaded, i * 32 + 32)
                need(pe, exp_done, i * NPAIR + (u - 1))
                m = maskT_first if i.k is None and i.b == 0 else maskT[:]
                if u not in MASKED:
                    nc.tensor.matmul(st_ps[u % 2].rearrange("p (h f) t -> p h (f t)", h=2), ident_b[:],
                                     m.rearrange("p f t -> p (f t)").unsqueeze(1).to_broadcast([128, 2, 2 * W]),
                                     start=True, stop=False, skip_group_check=True)
                for h in range(2):
                    for f in range(2):
                        at = k_at(s, b) + f * W
                        ins = nc.tensor.matmul(st_ps[u % 2][:, 2 * h + f],
                                               k_stack[0:KROWS + 2, 2 * u + h, at:at + W],
                                               q_stack[0:KROWS + 2, s.parity, 2 * u + h, b * W:(b + 1) * W],
                                               start=(u in MASKED and h == 0 and f == 0), stop=True, skip_group_check=True)
                ins.then_inc(st_full, 1)

            def weigh_values(s, b, g, i):
                if g == 0:
                    need(pe, v_ready, i + 1)
                if g == 0 and i.k is None and i.b == 0:
                    pe.wait_ge(heads_zeroed, 1)
                if g % 4 == 0:
                    need(pe, heads_copied, i * 2 + (g // 4 - 1))
                need(pe, exp_done, i * NPAIR + (2 * g + 2))
                for f in range(2):
                    for q in range(4):
                        h = 4 * g + q
                        ins = nc.tensor.matmul(heads_ps[g // 4][32 * q:32 * q + HR, g % 4, :],
                                               v_tok[:, 2 * s.parity + b + f, h, :],
                                               probs[:, (h // 2) % RING, 2 * (h % 2) + f, :],
                                               start=(f == 0), stop=(f == 1), skip_group_check=True)
                ins.then_inc(pv_done, 1)

            def body(s):
                t = s + 1
                for b in range(2):
                    i = s * 2 + b
                    tail, attend, score = (i - 1).within(0, NB), i.within(0, NB), (i + 1).within(0, NB)
                    proj = t.within(0, NS)
                    if proj and b == 0:
                        x_to_features(s, 0)
                        x_to_features(s, 1)
                    if proj and b == 1:
                        project_v(s, 0, 0, KT // 2)
                    if tail:
                        weigh_values(s if b else s - 1, (b + 1) % 2, 7, i - 1)
                    if proj and b == 0:
                        project_qk(s, 0)
                    if proj and b == 1:
                        project_v(s, 0, KT // 2, KT)
                    if tail:
                        heads_to_tokens(s, b, 1, i - 1)
                    if proj and b == 0:
                        project_qk(s, 1)
                    if proj and b == 1:
                        project_v(s, 1, 0, KT // 2)
                    if tail:
                        attn_to_features(s, b, i - 1)
                    if proj and b == 0:
                        project_qk(s, 2)
                    if proj and b == 1:
                        project_v(s, 1, KT // 2, KT)
                        if s.k is None and s.b == -1:
                            last_rows()
                    if tail:
                        project_out(s, b, i - 1)
                    if proj and b == 0:
                        project_qk(s, 3)
                    for u in range(NPAIR):
                        if attend:
                            scores_transposed(s, b, u, i)
                        if score and u < NSG:
                            scores(s, b, u, i + 1)
                        if attend and u % 2 and u >= 3:
                            weigh_values(s, b, (u - 3) // 2, i)
                        if attend and u == 13:
                            heads_to_tokens(s, b, 0, i)
                    if score:
                        bank = take_bank(pe, s, "mT", b, 0)
                        need(pe, max_done, (i + 2) * NSG)
                        nc.tensor.transpose(bank[0:H, 0:W], row_max[:], ident_f[:]).then_inc(mT_full, 1)

            turns(pe, body)

        first_phase.close()
        block = ctx.enter_context(nc.Block())
        taken = [2 * 2 * KT * D]

        def carve(elems, dt, pattern=None, **sizes):
            size = elems * (2 if dt == fp32 or dt == u32 else 1)
            piece = stacks[:, taken[0]:taken[0] + size]
            taken[0] += size
            piece = piece if dt == bf16 else piece.bitcast(dt)
            return piece.rearrange(pattern, **sizes) if pattern else piece

        wf_unit = carve(KT * D, fp32)
        wf_magic = carve(KT * D, fp32)
        wf_q = carve(KT * D, bf16, "p (k d) -> p k d", k=KT)
        wf_qT = carve(KT * D, bf16, "p (k d) -> p k d", k=KT)
        bias_part = carve(3 * D, bf16, "p (a d) -> p a d", a=3)
        bias_rows = carve(D, bf16)
        ones_rows = carve(128, bf16)
        ratio = carve(16, fp32)
        magic = carve(4 * D, fp32, "p (r d) -> p r d", r=4)
        hq = carve(4 * D, bf16, "p (r d) -> p r d", r=4)
        hqT = carve(4 * KT * W, bf16, "p (r k t) -> p r k t", r=4, k=KT)
        result = carve(4 * D, fp32, "p (r d) -> p r d", r=4)

        amax_own = sem("amax_own")
        amax_ready = sem("amax_ready")
        prep = sem("prep")
        scales_ready = sem("scales_ready")
        wf_unit_ready = sem("wf_unit_ready")
        wf_magic_ready = sem("wf_magic_ready")
        wf_rounded = sem("wf_rounded")
        wf_ready = sem("wf_ready")
        wfT_full = sem("wfT_full")
        wfT_ready = sem("wfT_ready")
        bias_ready = sem("bias_ready")
        unit_ready = sem("unit_ready")
        power_ready = sem("power_ready")
        magic_ready = sem("magic_ready")
        rounded_ready = sem("rounded_ready")
        hq_ready = sem("hq_ready")
        hqT_full = sem("hqT_full")
        hqT_ready = sem("hqT_ready")
        z_full = sem("z_full")
        z_scaled = sem("z_scaled")
        result_ready = [sem("result_ready_pool"), sem("result_ready_dve")]
        result_stored = [sem(f"result_stored_{r}") for r in range(4)]

        EXPONENT, SMALLEST, MAGIC = 0x7F800000, 2.0 ** -6, 1.5 * 2.0 ** 20

        def rounds(eng, body):
            for n in range(8):
                body(Count(None, 0, n))
            with eng.Fori(0, (NB - 12) // 4) as k:
                for n in range(8, 12):
                    body(Count(k, 4, n))
            for n in range(NB - 4, NB + 5):
                body(Count(None, 0, n))

        def fills(n):
            return (n - n.slot).over(4)

        hqT_ps = [ps[:, r, 0:KT * W // 2].bitcast(bf16).rearrange("p (k t) -> p k t", k=KT) for r in range(4)]
        z_ps = [ps[:, 4 + r, :] for r in range(4)]
        wfT_ps = [ps[:, 4 + k, 0:D // 2].bitcast(bf16) for k in range(KT)]

        def finish(ops, eng, n):
            need(eng, z_scaled, n + 1)
            need(eng, x1_back[n.slot], fills(n) * 16 + 16)
            ops.tensor_tensor(result[:, n.slot], result[:, n.slot], x1_in[:, n.slot], ALU.add).then_inc(result_ready[n.slot // 3], 1)

        def results(n):
            return fills(n) + 1 if n.slot == 3 else fills(n) * 3 + (n.slot + 1)

        @block.sync
        def _(sp):
            def load_h2(n):
                need(sp, hq_ready, n - 3, apart=True)
                sp.dma_start(h2_in[:, n.slot], h2_dram[bass.ds(n.value(), 1)].rearrange("a p d -> p (a d)")
                             ).then_inc(h2_loaded[n.slot], 16)

            def load_x1(n):
                if not (n.k is None and n.b < 4):
                    need(sp, result_ready[n.slot // 3], results(n - 4), apart=True)
                sp.dma_start(x1_in[:, n.slot], x1_dram[bass.ds(n.value(), 1)].rearrange("a p d -> p (a d)")
                             ).then_inc(x1_back[n.slot], 16)

            def store(n):
                need(sp, result_ready[n.slot // 3], results(n), apart=True)
                sp.dma_start(ob[bass.ds(n.value(), 1)].rearrange("a p d -> p (a d)"), result[:, n.slot]
                             ).then_inc(result_stored[n.slot], 16)

            def body(n):
                if (n + 2).within(4, NB):
                    load_h2(n + 2)
                if (n - 5).within(0, NB):
                    store(n - 5)
                if (n - 1).within(0, NB):
                    load_x1(n - 1)

            rounds(sp, body)
            for r in range(4):
                sp.wait_ge(result_stored[r], 16 * (NB // 4))

        @block.gpsimd
        def _(pool):
            pool.wait_ge(amax_own, 1)
            nc.gpsimd.partition_all_reduce(q8[:, 2:4], q8[:, 0:2], 128, bass.bass_isa.ReduceOp.max).then_inc(amax_ready, 1)

            def round_up(n):
                need(pool, magic_ready, n + 1)
                nc.gpsimd.tensor_tensor(h2_in[:, n.slot], h2_in[:, n.slot], magic[:, n.slot], ALU.add).then_inc(rounded_ready, 1)

            def body(n):
                if n.within(0, NB):
                    round_up(n)
                if n.k is None and n.b == 0:
                    pool.wait_ge(wf_magic_ready, 1)
                    nc.gpsimd.tensor_tensor(wf_unit, wf_unit, wf_magic, ALU.add).then_inc(wf_rounded, 1)
                if (n - 3).within(0, NB) and (n - 3).slot != 3:
                    finish(nc.gpsimd, pool, n - 3)

            rounds(pool, body)

        @block.scalar
        def _(act):
            act.wait_ge(scales_ready, 1)

            def units(n):
                need(act, h2_loaded[n.slot], fills(n) * 16 + 16)
                nc.scalar.activation(h2_in[:, n.slot], h2_in[:, n.slot], ACT.Copy, scale=q8[:, 6:7]).then_inc(unit_ready, 1)

            def turn_over(n):
                need(act, hqT_full, n + 1)
                nc.scalar.activation(hqT[:, n.slot], hqT_ps[n.slot], ACT.Copy).then_inc(hqT_ready, 1)

            def body(n):
                if n.within(0, NB):
                    units(n)
                if n.k is None and n.b == 0:
                    nc.scalar.activation(wf_unit, wf, ACT.Copy, scale=q8[:, 7:8]).then_inc(wf_unit_ready, 1)
                if n.k is None and n.b == 2:
                    for k in range(KT):
                        act.wait_ge(wfT_full, k + 1)
                        nc.scalar.activation(wf_qT[:, k], wfT_ps[k], ACT.Copy).then_inc(wfT_ready, 1)
                if (n - 2).within(0, NB):
                    turn_over(n - 2)

            rounds(act, body)

        @block.vector
        def _(dve):
            done = [0]

            def link(ins):
                done[0] += 1
                ins.then_inc(prep, 1)
                dve.wait_ge(prep, done[0])

            nc.vector.tensor_reduce(q8[:, 0:1], h2_max[:], AX, ALU.max).then_inc(amax_own, 1)
            dve.wait_ge(amax_ready, 1)
            link(nc.vector.tensor_tensor(q8[:, 3:4], q8[:, 3:4], q8[:, 2:3], ALU.max))
            link(nc.vector.tensor_scalar(q8[:, 4:6], q8[:, 2:4], 1.0 / QMAX, None, ALU.mult))
            link(nc.vector.reciprocal(q8[:, 6:8], q8[:, 4:6]))
            link(nc.vector.tensor_tensor(ratio[:, 0:1], q8[:, 4:5], q8[:, 5:6], ALU.mult))
            nc.vector.tensor_tensor(ratio[:, 1:2], q8[:, 6:7], q8[:, 7:8], ALU.mult).then_inc(scales_ready, 1)
            dve.wait_ge(scales_ready, 1)

            def powers(n):
                p = n.slot
                need(dve, unit_ready, n + 1)
                nc.vector.tensor_scalar(magic[:, p].bitcast(u32), h2_in[:, p].bitcast(u32), EXPONENT, None, ALU.bitwise_and).then_inc(power_ready, 1)
                need(dve, power_ready, n + 1)
                nc.vector.tensor_scalar(magic[:, p], magic[:, p], SMALLEST, MAGIC, ALU.max, ALU.mult).then_inc(magic_ready, 1)

            def grid(n):
                p = n.slot
                need(dve, rounded_ready, n + 1)
                need(dve, hqT_full, n - 3)
                nc.vector.tensor_tensor(hq[:, p], h2_in[:, p], magic[:, p], ALU.subtract).then_inc(hq_ready, 1)

            def scaled(n):
                p = n.slot
                need(dve, z_full, n + 1)
                need(dve, result_stored[p], fills(n) * 16)
                nc.vector.tensor_tensor(result[:, p], z_ps[p], gb_row[:], ALU.mult).then_inc(z_scaled, 1)

            def weight():
                dve.wait_ge(wf_unit_ready, 1)
                link(nc.vector.tensor_scalar(wf_magic.bitcast(u32), wf_unit.bitcast(u32), EXPONENT, None, ALU.bitwise_and))
                nc.vector.tensor_scalar(wf_magic, wf_magic, SMALLEST, MAGIC, ALU.max, ALU.mult).then_inc(wf_magic_ready, 1)

            def weight_grid():
                dve.wait_ge(wf_rounded, 1)
                nc.vector.tensor_tensor(wf_q.rearrange("p k d -> p (k d)"), wf_unit, wf_magic, ALU.subtract).then_inc(wf_ready, 1)

            def rows():
                link(nc.vector.tensor_scalar(gb_row[:], gb_row[:], ratio[:, 0:1], None, ALU.mult))
                link(nc.vector.tensor_scalar(bias_all, bias_all, ratio[:, 1:2], None, ALU.mult))
                for a in range(3):
                    link(nc.vector.tensor_copy(bias_part[:, a], bias_all))
                    if a < 2:
                        link(nc.vector.tensor_tensor(bias_all, bias_all, bias_part[:, a], ALU.subtract))
                link(nc.vector.memset(bias_rows, 0.0))
                link(nc.vector.memset(ones_rows, 1.0))
                for a in range(3):
                    ins = nc.vector.tensor_copy(bias_rows[32 * a:32 * a + 1], bias_part[32 * a:32 * a + 1, a])
                ins.then_inc(bias_ready, 1)

            def body(n):
                if n.within(0, NB):
                    powers(n)
                if n.k is None and n.b == 0:
                    weight()
                if n.k is None and n.b == 1:
                    rows()
                if (n - 1).within(0, NB):
                    grid(n - 1)
                if n.k is None and n.b == 1:
                    weight_grid()
                if (n - 3).within(0, NB):
                    scaled(n - 3)
                if (n - 4).within(0, NB) and n.slot == 3:
                    finish(nc.vector, dve, n - 4)

            rounds(dve, body)

        @block.tensor
        def _(pe):
            pe.wait_ge(wf_ready, 1)
            for k in range(KT):
                for o in range(KT):
                    ins = nc.tensor.transpose(wfT_ps[k][:, o * 128:(o + 1) * 128], wf_q[:, o, k * 128:(k + 1) * 128], ident_b[:])
                ins.then_inc(wfT_full, 1)

            def transposed(n):
                need(pe, hq_ready, n + 1)
                need(pe, hqT_ready, n - 3)
                for k in range(KT):
                    ins = nc.tensor.transpose(hqT_ps[n.slot][:, k], hq[:, n.slot, k * 128:(k + 1) * 128], ident_b[:])
                ins.then_inc(hqT_full, 1)

            def product(n):
                need(pe, hqT_ready, n + 1)
                need(pe, z_scaled, n - 3)
                for k in range(KT):
                    nc.tensor.matmul(z_ps[n.slot], hqT[:, n.slot, k], wf_qT[:, k], start=(k == 0), stop=False)
                nc.tensor.matmul(z_ps[n.slot], ones_rows[0:96], bias_rows[0:96], start=False, stop=True).then_inc(z_full, 1)

            def body(n):
                if n.within(0, NB):
                    transposed(n)
                if n.k is None and n.b == 1:
                    pe.wait_ge(wfT_ready, KT)
                    pe.wait_ge(bias_ready, 1)
                if (n - 1).within(0, NB):
                    product(n - 1)

            rounds(pe, body)


_INS = ['L0_attn_x', 'L0_attn_Wq', 'L0_attn_Wk', 'L0_attn_Wv', 'L0_attn_Wo', 'L0_ffn_weight', 'L0_ffn_bias', 'L0_c', 'L0_wmod']
_OUTS = [((1, 4096, 512), 'float32')]


def kernel(**inputs):
    import numpy as _np
    import concourse.bacc as _bacc
    from concourse import mybir as _mybir
    from concourse.bass_utils import run_bass_kernel_spmd as _run

    nc = _bacc.Bacc("TRN2", target_bir_lowering=False, num_devices=1)
    arrays, args = {}, []
    for name in _INS:
        a = _np.ascontiguousarray(inputs[name])
        arrays[f"in_{name}_dram"] = a
        args.append(nc.dram_tensor(f"in_{name}_dram", a.shape, _mybir.dt.from_np(a.dtype), kind="ExternalInput").ap())
    for i, (shape, dtype) in enumerate(_OUTS):
        dt = _mybir.dt.from_np(_np.dtype(dtype))
        args.append(nc.dram_tensor(f"out_{i}_dram", shape, dt, kind="ExternalOutput").ap())
    adaln_block(nc, *args)
    r = _run(nc, [arrays], core_ids=[0])
    return r.results[0]["out_0_dram"]
```
